# Optimizing a Trainium2 kernel written in Bass

```python
import numpy as np
import jax
import jax.numpy as jnp

def _softmax(x, axis=-1):
    return jax.nn.softmax(x, axis=axis)

def _gelu(x):
    return jax.nn.gelu(x, approximate=True)

def _silu(x):
    return jax.nn.silu(x)

def _sigmoid(x):
    return jax.nn.sigmoid(x)

def _layernorm(x, axis=-1, eps=1e-05):
    m = jnp.mean(x, axis=axis, keepdims=True)
    v = jnp.var(x, axis=axis, keepdims=True)
    return (x - m) / jnp.sqrt(v + eps)

def _scatter_add(tgt, idx, src, axis=0):
    return tgt.at[idx].add(src)

def _segment_sum(src, seg, n):
    return jax.ops.segment_sum(src, seg, n)
kernel_name = 'mk_dlrm_tower_d1_rec_r8_a10dfa'

def setup_inputs(seed: int=0):
    np.random.seed(seed)
    _w = jnp.asarray

    def _rec_inputs():
        import jax
        import jax.numpy as jnp
        _tk = jax.random.key(seed)
        dense_ctx = jax.random.normal(jax.random.fold_in(_tk, 190), (1024, 16), jnp.float32)
        ids = jnp.stack([jax.random.randint(jax.random.fold_in(_tk, 200 + f), (1024,), 0, v, jnp.int32) for f, v in enumerate([12500, 125000, 125000, 12500, 1250, 125000, 1250, 1000, 1000, 12500, 1000, 1000, 12500, 1250, 1000, 1250, 1000, 125000, 1250, 1250, 125000, 1000, 125000, 1250, 1000, 12500, 1000, 1250, 1250, 1250, 1250, 125000])], axis=1)
        tbl_0 = 0.05 * jax.random.normal(jax.random.fold_in(_tk, 500 + 0), (12500, 32), jnp.float32)
        tbl_1 = 0.05 * jax.random.normal(jax.random.fold_in(_tk, 500 + 1), (125000, 32), jnp.float32)
        tbl_2 = 0.05 * jax.random.normal(jax.random.fold_in(_tk, 500 + 2), (125000, 32), jnp.float32)
        tbl_3 = 0.05 * jax.random.normal(jax.random.fold_in(_tk, 500 + 3), (12500, 32), jnp.float32)
        tbl_4 = 0.05 * jax.random.normal(jax.random.fold_in(_tk, 500 + 4), (1250, 32), jnp.float32)
        tbl_5 = 0.05 * jax.random.normal(jax.random.fold_in(_tk, 500 + 5), (125000, 32), jnp.float32)
        tbl_6 = 0.05 * jax.random.normal(jax.random.fold_in(_tk, 500 + 6), (1250, 32), jnp.float32)
        tbl_7 = 0.05 * jax.random.normal(jax.random.fold_in(_tk, 500 + 7), (1000, 32), jnp.float32)
        tbl_8 = 0.05 * jax.random.normal(jax.random.fold_in(_tk, 500 + 8), (1000, 32), jnp.float32)
        tbl_9 = 0.05 * jax.random.normal(jax.random.fold_in(_tk, 500 + 9), (12500, 32), jnp.float32)
        tbl_10 = 0.05 * jax.random.normal(jax.random.fold_in(_tk, 500 + 10), (1000, 32), jnp.float32)
        tbl_11 = 0.05 * jax.random.normal(jax.random.fold_in(_tk, 500 + 11), (1000, 32), jnp.float32)
        tbl_12 = 0.05 * jax.random.normal(jax.random.fold_in(_tk, 500 + 12), (12500, 32), jnp.float32)
        tbl_13 = 0.05 * jax.random.normal(jax.random.fold_in(_tk, 500 + 13), (1250, 32), jnp.float32)
        tbl_14 = 0.05 * jax.random.normal(jax.random.fold_in(_tk, 500 + 14), (1000, 32), jnp.float32)
        tbl_15 = 0.05 * jax.random.normal(jax.random.fold_in(_tk, 500 + 15), (1250, 32), jnp.float32)
        tbl_16 = 0.05 * jax.random.normal(jax.random.fold_in(_tk, 500 + 16), (1000, 32), jnp.float32)
        tbl_17 = 0.05 * jax.random.normal(jax.random.fold_in(_tk, 500 + 17), (125000, 32), jnp.float32)
        tbl_18 = 0.05 * jax.random.normal(jax.random.fold_in(_tk, 500 + 18), (1250, 32), jnp.float32)
        tbl_19 = 0.05 * jax.random.normal(jax.random.fold_in(_tk, 500 + 19), (1250, 32), jnp.float32)
        tbl_20 = 0.05 * jax.random.normal(jax.random.fold_in(_tk, 500 + 20), (125000, 32), jnp.float32)
        tbl_21 = 0.05 * jax.random.normal(jax.random.fold_in(_tk, 500 + 21), (1000, 32), jnp.float32)
        tbl_22 = 0.05 * jax.random.normal(jax.random.fold_in(_tk, 500 + 22), (125000, 32), jnp.float32)
        tbl_23 = 0.05 * jax.random.normal(jax.random.fold_in(_tk, 500 + 23), (1250, 32), jnp.float32)
        tbl_24 = 0.05 * jax.random.normal(jax.random.fold_in(_tk, 500 + 24), (1000, 32), jnp.float32)
        tbl_25 = 0.05 * jax.random.normal(jax.random.fold_in(_tk, 500 + 25), (12500, 32), jnp.float32)
        tbl_26 = 0.05 * jax.random.normal(jax.random.fold_in(_tk, 500 + 26), (1000, 32), jnp.float32)
        tbl_27 = 0.05 * jax.random.normal(jax.random.fold_in(_tk, 500 + 27), (1250, 32), jnp.float32)
        tbl_28 = 0.05 * jax.random.normal(jax.random.fold_in(_tk, 500 + 28), (1250, 32), jnp.float32)
        tbl_29 = 0.05 * jax.random.normal(jax.random.fold_in(_tk, 500 + 29), (1250, 32), jnp.float32)
        tbl_30 = 0.05 * jax.random.normal(jax.random.fold_in(_tk, 500 + 30), (1250, 32), jnp.float32)
        tbl_31 = 0.05 * jax.random.normal(jax.random.fold_in(_tk, 500 + 31), (125000, 32), jnp.float32)
        _rk = jax.random.fold_in(_tk, 7)
        W_top1 = 0.0606339 * jax.random.normal(jax.random.fold_in(_tk, 801), (272, 512), jnp.float32)
        W_top2 = 0.0441942 * jax.random.normal(jax.random.fold_in(_tk, 802), (512, 256), jnp.float32)
        W_top3 = 0.0625 * jax.random.normal(jax.random.fold_in(_tk, 803), (256, 1), jnp.float32)
        b_top1 = jnp.zeros((512,), jnp.float32)
        b_top2 = jnp.zeros((256,), jnp.float32)
        return (dense_ctx, ids, tbl_0, tbl_1, tbl_2, tbl_3, tbl_4, tbl_5, tbl_6, tbl_7, tbl_8, tbl_9, tbl_10, tbl_11, tbl_12, tbl_13, tbl_14, tbl_15, tbl_16, tbl_17, tbl_18, tbl_19, tbl_20, tbl_21, tbl_22, tbl_23, tbl_24, tbl_25, tbl_26, tbl_27, tbl_28, tbl_29, tbl_30, tbl_31, W_top1, b_top1, W_top2, b_top2, W_top3)
    dense_ctx, ids, tbl_0, tbl_1, tbl_2, tbl_3, tbl_4, tbl_5, tbl_6, tbl_7, tbl_8, tbl_9, tbl_10, tbl_11, tbl_12, tbl_13, tbl_14, tbl_15, tbl_16, tbl_17, tbl_18, tbl_19, tbl_20, tbl_21, tbl_22, tbl_23, tbl_24, tbl_25, tbl_26, tbl_27, tbl_28, tbl_29, tbl_30, tbl_31, W_top1, b_top1, W_top2, b_top2, W_top3 = _rec_inputs()

    def _L0_rec_setup():
        import jax, jax.numpy as jnp
        import numpy as np
        B, N, K = (256, 32, 32)
        CIN_SIZE = [128, 128]
        key = jax.random.key(seed)
        k1, k2, k3 = jax.random.split(key, 3)
        inputs = jax.random.normal(k1, (B, N, K), dtype=jnp.float32)
        W0 = jax.random.normal(k2, (N * N, CIN_SIZE[0]), dtype=jnp.float32) * 0.04
        W1 = jax.random.normal(k3, (N * CIN_SIZE[0], CIN_SIZE[1]), dtype=jnp.float32) * 0.02
        return {'inputs': inputs, 'W0': W0, 'W1': W1}
    _L0_rec_all = _L0_rec_setup()
    _L0_rec_in = {k: v for k, v in _L0_rec_all.items() if k in ('W0', 'W1')}
    del _L0_rec_all
    return {'dense_ctx': dense_ctx, 'ids': ids, 'tbl_0': tbl_0, 'tbl_1': tbl_1, 'tbl_2': tbl_2, 'tbl_3': tbl_3, 'tbl_4': tbl_4, 'tbl_5': tbl_5, 'tbl_6': tbl_6, 'tbl_7': tbl_7, 'tbl_8': tbl_8, 'tbl_9': tbl_9, 'tbl_10': tbl_10, 'tbl_11': tbl_11, 'tbl_12': tbl_12, 'tbl_13': tbl_13, 'tbl_14': tbl_14, 'tbl_15': tbl_15, 'tbl_16': tbl_16, 'tbl_17': tbl_17, 'tbl_18': tbl_18, 'tbl_19': tbl_19, 'tbl_20': tbl_20, 'tbl_21': tbl_21, 'tbl_22': tbl_22, 'tbl_23': tbl_23, 'tbl_24': tbl_24, 'tbl_25': tbl_25, 'tbl_26': tbl_26, 'tbl_27': tbl_27, 'tbl_28': tbl_28, 'tbl_29': tbl_29, 'tbl_30': tbl_30, 'tbl_31': tbl_31, 'W_top1': W_top1, 'b_top1': b_top1, 'W_top2': W_top2, 'b_top2': b_top2, 'W_top3': W_top3, 'L0_rec_W0': _L0_rec_in['W0'], 'L0_rec_W1': _L0_rec_in['W1']}

def reference(dense_ctx, ids, tbl_0, tbl_1, tbl_2, tbl_3, tbl_4, tbl_5, tbl_6, tbl_7, tbl_8, tbl_9, tbl_10, tbl_11, tbl_12, tbl_13, tbl_14, tbl_15, tbl_16, tbl_17, tbl_18, tbl_19, tbl_20, tbl_21, tbl_22, tbl_23, tbl_24, tbl_25, tbl_26, tbl_27, tbl_28, tbl_29, tbl_30, tbl_31, W_top1, b_top1, W_top2, b_top2, W_top3, L0_rec_W0, L0_rec_W1):
    import jax
    import jax.numpy as jnp

    def _L0_rec_ref(inputs, W0, W1):
        import jax, jax.numpy as jnp
        import numpy as np
        B, N, K = (256, 32, 32)
        CIN_SIZE = [128, 128]
        b, n, k = inputs.shape
        x = inputs
        res = []
        for W in (W0, W1):
            prev = x.shape[1]
            z = jnp.einsum('bhd,bmd->bhmd', inputs, x).reshape(b, n * prev, k)
            x = jnp.einsum('bpd,pj->bjd', z, W)
            res.append(x)
        out = jnp.sum(jnp.concatenate(res, axis=1), axis=-1)
        return out
    e = jnp.stack([tbl_0[ids[:, 0]], tbl_1[ids[:, 1]], tbl_2[ids[:, 2]], tbl_3[ids[:, 3]], tbl_4[ids[:, 4]], tbl_5[ids[:, 5]], tbl_6[ids[:, 6]], tbl_7[ids[:, 7]], tbl_8[ids[:, 8]], tbl_9[ids[:, 9]], tbl_10[ids[:, 10]], tbl_11[ids[:, 11]], tbl_12[ids[:, 12]], tbl_13[ids[:, 13]], tbl_14[ids[:, 14]], tbl_15[ids[:, 15]], tbl_16[ids[:, 16]], tbl_17[ids[:, 17]], tbl_18[ids[:, 18]], tbl_19[ids[:, 19]], tbl_20[ids[:, 20]], tbl_21[ids[:, 21]], tbl_22[ids[:, 22]], tbl_23[ids[:, 23]], tbl_24[ids[:, 24]], tbl_25[ids[:, 25]], tbl_26[ids[:, 26]], tbl_27[ids[:, 27]], tbl_28[ids[:, 28]], tbl_29[ids[:, 29]], tbl_30[ids[:, 30]], tbl_31[ids[:, 31]]], axis=1)
    z = _L0_rec_ref(e, L0_rec_W0, L0_rec_W1)
    z = z.reshape(z.shape[0], -1)
    h = jnp.concatenate([z, dense_ctx], axis=1)
    h = jnp.maximum(h @ W_top1 + b_top1, 0.0)
    h = jnp.maximum(h @ W_top2 + b_top2, 0.0)
    y = h @ W_top3
    return y

_drawn_inputs = setup_inputs


def setup_inputs(seed=0):
    import zlib

    import numpy as np

    out = dict(_drawn_inputs(seed))
    spreads = {'b_top1': (0.0, 0.1), 'b_top2': (0.0, 0.1)}
    factors = {'tbl_0': 4.61,
     'tbl_1': 4.969,
     'tbl_2': 4.815,
     'tbl_3': 5.208,
     'tbl_4': 4.885,
     'tbl_5': 4.97,
     'tbl_6': 4.971,
     'tbl_7': 5.186,
     'tbl_8': 5.024,
     'tbl_9': 4.932,
     'tbl_10': 4.631,
     'tbl_11': 5.052,
     'tbl_12': 5.215,
     'tbl_13': 4.79,
     'tbl_14': 4.898,
     'tbl_15': 4.766,
     'tbl_16': 5.259,
     'tbl_17': 5.055,
     'tbl_18': 5.463,
     'tbl_19': 5.092,
     'tbl_20': 4.78,
     'tbl_21': 4.988,
     'tbl_22': 5.023,
     'tbl_23': 5.026,
     'tbl_24': 5.037,
     'tbl_25': 4.935,
     'tbl_26': 4.587,
     'tbl_27': 5.153,
     'tbl_28': 5.121,
     'tbl_29': 5.042,
     'tbl_30': 4.735,
     'tbl_31': 4.638,
     'L0_rec_W1': 8.0}
    for name, (base, spread) in spreads.items():
        noise = np.random.default_rng([zlib.crc32(name.encode()), seed]).standard_normal(out[name].shape)
        drawn = base * np.exp(spread * noise) if base else spread * noise
        out[name] = jnp.asarray(drawn.astype(out[name].dtype))
    for name, factor in factors.items():
        out[name] = (out[name] * factor).astype(out[name].dtype)
    return out
```

```python
import concourse.bass as bass
from concourse import mybir
from contextlib import ExitStack

F32 = mybir.dt.float32
F32R = mybir.dt.float32r
I32 = mybir.dt.int32
ALU = mybir.AluOpType
ACT = mybir.ActivationFunctionType
AX = mybir.AxisListType


def dlrm_cin_tower(nc, dense_ctx, ids, tables, w_top1, b_top1, w_top2, b_top2, w_top3, w0, w1, out):
    B, F = ids.shape
    D = tables[0].shape[1]
    P = 128
    J = w0.shape[1]
    ND = dense_ctx.shape[1]
    H1, H2 = w_top1.shape[1], w_top2.shape[1]
    TILES = B // P
    NQ = P // F
    SHIFT_TILES = 4
    HALF = F // 2
    CD = 4
    CHUNKS = D // CD
    SUPERS = CHUNKS // 2
    BANK = 512
    UNITS = 8
    GROUPS = P // NQ
    GU = GROUPS // UNITS
    EU = 2
    MOVES = EU * NQ * NQ
    KT1 = 2
    N1, N2 = H1 // P, H2 // P
    assert CD * P == BANK and GU * P == BANK and F * NQ == P and D == F and J == P

    ctx = ExitStack()
    with ctx:
        def sb(name, shape, dt=F32):
            return ctx.enter_context(nc.sbuf_tensor(name, shape, dt))

        def ps(name, shape):
            return ctx.enter_context(nc.psum_tensor(name, shape, F32))

        def sem(name):
            return ctx.enter_context(nc.semaphore(name))

        def view(ap, free):
            return bass.AP(ap.tensor, ap.offset, [list(ap.ap[0])] + [list(x) for x in free])

        ident = sb("ident", [P, P])
        ident32 = sb("ident32", [P, 2 * F])
        quad = sb("quad", [P, NQ])
        oct_ = sb("oct", [P, 8])
        half32 = sb("half32", [P, 2])
        half16 = sb("half16", [P, 2])
        sel = sb("sel", [P, 5, 2, P], F32R)
        sel16 = sb("sel16", [P, 2, P], F32R)
        w0a = sb("w0a", [P, 5, J])
        w0b = sb("w0b", [P, 5, J])
        w0h = sb("w0h", [P, SHIFT_TILES, J], F32R)
        w0l = sb("w0l", [P, SHIFT_TILES, J], F32R)
        w16 = sb("w16", [P, J])
        w16h = sb("w16h", [P, J], F32R)
        w16m = sb("w16m", [P, 2, J], F32R)
        w1s = sb("w1s", [P, F, J])
        idc = [sb(f"idc{i}", [P, F], I32) for i in range(2)]
        emb = [sb(f"emb{i}", [P, F, D]) for i in range(2)]
        embd = [sb(f"embd{i}", [P, D, F]) for i in range(2)]
        S = [sb(f"S{i}", [P, BANK], F32R) for i in range(2)]
        e4 = [sb(f"e4{i}", [P, BANK]) for i in range(2)]
        b16 = sb("b16", [P, BANK])
        z = [sb(f"z{i}", [P, SHIFT_TILES, BANK]) for i in range(2)]
        zh = [sb(f"zh{i}", [P, SHIFT_TILES, BANK], F32R) for i in range(2)]
        zl = [sb(f"zl{i}", [P, SHIFT_TILES, BANK], F32R) for i in range(2)]
        z16 = sb("z16", [P, BANK])
        z16p = [sb(f"z16p{i}", [P, BANK], F32R) for i in range(2)]
        x1 = [sb(f"x1{i}", [P, P, D]) for i in range(2)]
        x1t = [sb(f"x1t{i}", [P, GU, P]) for i in range(2)]
        eblk = sb("eblk", [P, GROUPS, NQ, F])
        G = sb("G", [P, F, P])
        zf = sb("zf", [P, KT1, B])

        R = [ps(f"R{i}", [P, 2, BANK]) for i in range(2)]
        XO = ps("XO", [P, BANK])
        U0 = ps("U0", [P, BANK])
        U1 = ps("U1", [P, BANK])
        WA = ps("WA", [P, BANK])

        const_s = sem("const_s")
        masks_s = sem("masks_s")
        w0_loaded = sem("w0_loaded")
        w1_loaded = sem("w1_loaded")
        ids_loaded = [sem(f"ids_loaded{i}") for i in range(2)]
        gathered = [sem(f"gathered{i}") for i in range(2)]
        embd_done = sem("embd_done")
        s_transposed = sem("s_transposed")
        s_hi_done = sem("s_hi_done")
        s_lo_done = sem("s_lo_done")
        selected = sem("selected")
        e4_done = sem("e4_done")
        z_done = sem("z_done")
        zh_done = sem("zh_done")
        zl_done = sem("zl_done")
        zl3_done = sem("zl3_done")
        x1_made = sem("x1_made")
        x1_kept = sem("x1_kept")
        summed = sem("summed")
        e_transposed = sem("e_transposed")
        eblk_done = sem("eblk_done")
        x1_transposed = sem("x1_transposed")
        x1t_done = sem("x1t_done")
        g_made = sem("g_made")
        g_kept = sem("g_kept")
        x2_made = sem("x2_made")
        x2_kept = sem("x2_kept")

        def wait(eng, s, value):
            if not (isinstance(value, int) and value <= 0):
                eng.wait_ge(s, value)

        def unit(n, kind):
            return 7 * (n // 2) + ({"E4": 0, "R01": 1, "R23": 2, "REM": 3} if n % 2 == 0 else
                                   {"E4": 4, "R01": 5, "R23": 6})[kind]

        def zpos(n, kind):
            return 5 * (n // 2) + ({"01": 0, "23": 1, "16": 2} if n % 2 == 0 else {"01": 3, "23": 4})[kind]

        def e4pos(n, kind):
            return 3 * (n // 2) + ({"E4": 0, "B16": 1} if n % 2 == 0 else {"E4": 2})[kind]

        SEL, ZS, E4S = 7 * SUPERS, 5 * SUPERS, 3 * SUPERS

        G_UNITS = {n: (2 * (n - 1), 2 * (n - 1) + 1) for n in range(1, 5)}
        E_UNITS = {5: 0, 6: 1}
        X2_FIELDS = {5: range(0, 10), 6: range(10, 21), 7: range(21, F)}
        GATHERS = {0: 5, 1: 5, 2: 5, 3: 5, 4: 4, 5: 4, 6: 4}

        def tiles(eng, body, last_extra=True):
            body(0, 0, 0, True, False)
            with eng.Fori(0, (TILES - 2) // 2) as i:
                body(2 * i + 1, 1, i, False, False)
                body(2 * i + 2, 0, i + 1, False, False)
            body(TILES - 1, 1, (TILES - 1) // 2, False, False)
            if last_extra:
                body(TILES, 0, TILES // 2, False, True)

        HB = B // 2
        wt1 = emb[0][:, :, :].rearrange("p f d -> p (f d)").rearrange("p (t n) -> p t n", t=KT1)
        wt1d = sb("wt1d", [ND, H1])
        wt2 = emb[1][:, :, :].rearrange("p f d -> p (f d)").rearrange("p (t n) -> p t n", t=N1)
        vec_in = sb("vec_in", [N1 + N2 + N2, P])
        vec = sb("vec", [P, N1 + N2 + N2])
        dense_in = sb("dense_in", [P, TILES, ND])
        tower_loaded = sem("tower_loaded")
        vec_transposed = sem("vec_transposed")
        dense_transposed = sem("dense_transposed")
        tower_in = sem("tower_in")
        t_hi = sem("t_hi")
        t_lo = sem("t_lo")
        l1_made = sem("l1_made")
        l1_kept = sem("l1_kept")
        l1_hi = sem("l1_hi")
        l1_lo = sem("l1_lo")
        l2_made = sem("l2_made")
        l2_kept = sem("l2_kept")
        y_made = sem("y_made")
        y_kept = sem("y_kept")
        y_stored = sem("y_stored")

        wt1h = zh[0][:, 0:2, :]
        wt1l = zl[0][:, 0:2, :]
        wt2h = zh[0][:, 2:4, :].rearrange("p a (b n) -> p (a b) n", n=H2)
        wt2l = zl[0][:, 2:4, :].rearrange("p a (b n) -> p (a b) n", n=H2)
        wt1dh, wt1dl = z16p[0][0:ND, :], z16p[1][0:ND, :]
        dT = eblk[0:ND, :, :, :].rearrange("p a b c -> p (a b c)")[:, 0:B]
        dTh, dTl = S[0][0:ND, :], S[1][0:ND, :]
        zfh, zfl = sb("zfh", [P, KT1, HB], F32R), sb("zfl", [P, KT1, HB], F32R)
        h1, h1h, h1l = z[0], zh[1], zl[1]
        h2 = z[1][:, 0:N2, :]
        ybuf = [e4[0][0:1, :], e4[1][0:1, :]]
        W0_DMAS = 1 + 4 * (4 * SHIFT_TILES - 1) + 2 * (P // HALF)
        TOWER_DMAS = 7

        block = ctx.enter_context(nc.Block())

        @block.sync
        def _(eng):
            def ids_of(k, par, uses):
                wait(eng, gathered[par], 16 * F * uses)
                eng.dma_start(idc[par][:, :], ids[bass.ds(P * k, P), :]).then_inc(ids_loaded[par], 16)

            ids_of(0, 0, 0)
            ids_of(1, 1, 0)
            for s in range(4 * SHIFT_TILES):
                t, q = s // NQ, s % NQ
                for buf, step, at, wrap in ((w0a, F + 1, s, F), (w0b, F + 1, F * s, F * F)):
                    if s == 0 and buf is w0b:
                        continue
                    n = F - s
                    eng.dma_start(buf[F * q:F * q + n, t, :], w0[at:at + step * (n - 1) + 1:step, :])\
                       .then_inc(w0_loaded, 16)
                    if s:
                        first = at + step * n - wrap
                        eng.dma_start(buf[F * q + n:F * q + F, t, :],
                                      w0[first:first + step * (s - 1) + 1:step, :]).then_inc(w0_loaded, 16)
            for r in range(P // HALF):
                for buf, at in ((w0a, HALF), (w0b, F * HALF)):
                    eng.dma_start(buf[HALF * r:HALF * r + HALF, SHIFT_TILES, :],
                                  w0[at:at + (F + 1) * (HALF - 1) + 1:F + 1, :]).then_inc(w0_loaded, 16)
            eng.dma_start(w1s[:, :, :], w1.rearrange("(h m) j -> m h j", m=P)).then_inc(w1_loaded, 16)
            eng.dma_start(wt1d[:, :], w_top1[KT1 * P:KT1 * P + ND, :]).then_inc(tower_loaded, 16)
            eng.dma_start(vec_in[0:N1, :], b_top1.rearrange("(t p) -> t p", p=P)).then_inc(tower_loaded, 16)
            eng.dma_start(vec_in[N1:N1 + N2, :], b_top2.rearrange("(t p) -> t p", p=P)).then_inc(tower_loaded, 16)
            eng.dma_start(vec_in[N1 + N2:, :], w_top3.rearrange("(t p) o -> t (p o)", p=P)).then_inc(tower_loaded, 16)
            eng.dma_start(dense_in[:, :, :], dense_ctx.rearrange("(t p) n -> p t n", p=P)).then_inc(tower_loaded, 16)
            with eng.Fori(1, TILES // 2) as i:
                ids_of(2 * i, 0, i)
                ids_of(2 * i + 1, 1, i)
            eng.wait_ge(e_transposed, EU * (TILES - 1))
            eng.dma_start(wt1, w_top1[0:KT1 * P, :].rearrange("(t p) n -> p t n", p=P)).then_inc(tower_loaded, 16)
            eng.wait_ge(e_transposed, EU * TILES)
            eng.wait_ge(embd_done, TILES)
            eng.dma_start(wt2, w_top2.rearrange("(t p) n -> p t n", p=P)).then_inc(tower_loaded, 16)
            for hb in range(2):
                eng.wait_ge(y_kept, hb + 1)
                eng.dma_start(out[hb * HB:(hb + 1) * HB, :].rearrange("b o -> o b"), ybuf[hb]).then_inc(y_stored, 16)
            eng.wait_ge(y_stored, 32)

        @block.gpsimd
        def _(eng):
            eng.memset(ident[:, :], 0.0).then_inc(const_s, 1)
            eng.memset(ident32[:, :], 0.0).then_inc(const_s, 1)
            eng.memset(quad[:, :], 1.0).then_inc(const_s, 1)
            eng.memset(oct_[:, :], 1.0).then_inc(const_s, 1)
            eng.wait_ge(const_s, 4)
            eng.affine_select(out=ident[:, :], in_=ident[:, :], compare_op=ALU.not_equal, fill=1.0,
                              base=0, pattern=[[-1, P]], channel_multiplier=1).then_inc(const_s, 1)
            eng.affine_select(out=quad[:, :], in_=quad[:, :], compare_op=ALU.is_ge, fill=0.0,
                              base=0, pattern=[[-F, NQ]], channel_multiplier=1).then_inc(const_s, 1)
            eng.affine_select(out=oct_[:, :], in_=oct_[:, :], compare_op=ALU.is_ge, fill=0.0,
                              base=0, pattern=[[-HALF, 8]], channel_multiplier=1).then_inc(const_s, 1)
            eng.wait_ge(const_s, 7)
            eng.affine_select(out=quad[:, :], in_=quad[:, :], compare_op=ALU.is_ge, fill=0.0,
                              base=F - 1, pattern=[[F, NQ]], channel_multiplier=-1).then_inc(const_s, 1)
            eng.affine_select(out=oct_[:, :], in_=oct_[:, :], compare_op=ALU.is_ge, fill=0.0,
                              base=HALF - 1, pattern=[[HALF, 8]], channel_multiplier=-1).then_inc(const_s, 1)
            for a in range(NQ):
                eng.wait_ge(const_s, 9 + a)
                eng.affine_select(out=ident32[:, :].rearrange("p (c h) -> p c h", h=F),
                                  in_=ident32[:, :].rearrange("p (c h) -> p c h", h=F),
                                  compare_op=ALU.not_equal, fill=1.0, base=-F * a,
                                  pattern=[[0, 2], [-1, F]], channel_multiplier=1).then_inc(const_s, 1)

            def gather(k, par, uses, fields):
                for f in fields:
                    eng.indirect_dma_start(emb[par][:, f, :], None, tables[f],
                                           bass.IndirectOffsetOnAxis(idc[par][:, f:f + 1], 0))\
                       .then_inc(gathered[par], 16)

            eng.wait_ge(ids_loaded[0], 16)
            gather(0, 0, 0, range(F))

            def body(k, par, uses, first, last, more=True):
                f = 0
                for n in range(CHUNKS):
                    if more and n in GATHERS:
                        if n == 0:
                            eng.wait_ge(ids_loaded[1 - par], 16 * (uses + par + 1))
                            wait(eng, e_transposed, EU * k)
                            eng.nop(nofuse=True)
                        gather(k + 1, 1 - par, 0, range(f, f + GATHERS[n]))
                        f += GATHERS[n]
                    eng.wait_ge(zh_done, ZS * k + zpos(n, "23") + 1)
                    wait(eng, x1_made, CHUNKS * k + n - 1)
                    eng.tensor_tensor(zl[n % 2][:, 3, :], z[n % 2][:, 3, :], zh[n % 2][:, 3, :].bitcast(F32),
                                      ALU.subtract).then_inc(zl3_done, 1)

            body(0, 0, 0, True, False)
            with eng.Fori(0, (TILES - 2) // 2) as i:
                body(2 * i + 1, 1, i, False, False)
                body(2 * i + 2, 0, i + 1, False, False)
            body(TILES - 1, 1, (TILES - 1) // 2, False, False, more=False)

        @block.scalar
        def _(eng):
            def copy(dst, src):
                return eng.activation(dst, src, ACT.Copy)

            def by_d(k, par, uses):
                eng.wait_ge(gathered[par], 16 * F * (uses + 1))
                wait(eng, s_transposed, SUPERS * (k - 1))
                copy(embd[par][:, :, :], emb[par][:, :, :].rearrange("p f d -> p d f")).then_inc(embd_done, 1)

            def s_hi(k, sg):
                eng.wait_ge(s_transposed, SUPERS * k + sg + 1)
                wait(eng, selected, SEL * k + 7 * (sg - 1))
                copy(S[sg % 2][0:2 * F, :], U0[0:2 * F, :]).then_inc(s_hi_done, 1)

            def body(k, par, uses, first, last):
                for n in range(CHUNKS):
                    units = G_UNITS.get(n, ()) if not first else ()

                    def x1t_copy(u):
                        eng.wait_ge(x1_transposed, UNITS * (k - 1) + u + 1)
                        if u > 1:
                            eng.wait_ge(g_made, UNITS * (k - 1) + u - 1)
                        copy(x1t[u % 2][:, :, :], U1[:, :]).then_inc(x1t_done, 1)

                    def g_copy(u):
                        eng.wait_ge(g_made, UNITS * (k - 1) + u + 1)
                        copy(G[:, :, HALF * u:HALF * u + HALF],
                             U1[:, :].rearrange("p (b h) -> p h b", h=F)).then_inc(g_kept, 1)

                    if not last:
                        eng.wait_ge(selected, SEL * k + unit(n, "E4") + 1)
                        wait(eng, z_done, ZS * k + (zpos(n - 2, "23") + 1 if n >= 2 else zpos(n - 2 + CHUNKS, "23") + 1 - ZS))
                        copy(e4[n % 2][:, :], R[unit(n, "E4") % 2][:, 0, :]).then_inc(e4_done, 1)
                    if units:
                        x1t_copy(units[0])
                    if not last:
                        eng.wait_ge(z_done, ZS * k + zpos(n, "01") + 1)
                        wait(eng, x1_made, CHUNKS * k + n - 1)
                        copy(zh[n % 2][:, 0:2, :], z[n % 2][:, 0:2, :]).then_inc(zh_done, 1)
                    if units:
                        g_copy(units[0])
                    if not last:
                        eng.wait_ge(z_done, ZS * k + zpos(n, "23") + 1)
                        copy(zh[n % 2][:, 2:4, :], z[n % 2][:, 2:4, :]).then_inc(zh_done, 1)
                    if not (first and n == 0) and not (last and n > 0):
                        kk, m = (k, n - 1) if n else (k - 1, CHUNKS - 1)
                        pp = par if n else 1 - par
                        eng.wait_ge(x1_made, CHUNKS * kk + m + 1)
                        d = 2 * CD * (m // 2) + m % 2
                        copy(x1[pp][:, :, d:d + 2 * CD - 1:2],
                             XO[:, :].rearrange("p (d b) -> p b d", d=CD)).then_inc(x1_kept, 1)
                    if not last and n % 2 == 0:
                        eng.wait_ge(selected, SEL * k + unit(n, "REM") + 1)
                        wait(eng, z_done, ZS * k + zpos(n, "16") + 1 - 5)
                        copy(b16[:, :], R[unit(n, "REM") % 2][:, 0, :]).then_inc(e4_done, 1)
                    if not last and n in (0, 2, 4):
                        s_hi(k, n // 2 + 1)
                    if n == CHUNKS - 1 and not last and not (isinstance(k, int) and k == TILES - 1):
                        by_d(k + 1, 1 - par, uses + par)
                        s_hi(k + 1, 0)
                    if units:
                        x1t_copy(units[1])
                    if not last and n % 2 == 0:
                        eng.wait_ge(z_done, ZS * k + zpos(n, "16") + 1)
                        wait(eng, x1_made, CHUNKS * k + n - 2)
                        copy(z16p[n // 2 % 2][:, :], z16[:, :]).then_inc(zh_done, 1)
                    if units:
                        g_copy(units[1])
                    if n == CHUNKS - 1 and not first:
                        eng.wait_ge(x2_made, k)
                        copy(zf[:, 1, bass.ds(P * (k - 1), P)], WA[:, 0:P]).then_inc(x2_kept, 1)

            by_d(0, 0, 0)
            s_hi(0, 0)
            tiles(eng, body)

            eng.wait_ge(vec_transposed, 1)
            copy(vec[:, :], WA[:, 0:N1 + 2 * N2]).then_inc(tower_in, 1)
            for hb in range(2):
                eng.wait_ge(dense_transposed, hb + 1)
                copy(dT[:, hb * HB:(hb + 1) * HB], R[0][0:ND, hb, :]).then_inc(tower_in, 1)
            eng.wait_ge(tower_loaded, 16 * TOWER_DMAS)
            eng.wait_ge(x1_made, CHUNKS * TILES)
            copy(wt1h, wt1).then_inc(t_hi, 1)
            copy(wt1dh, wt1d[:, :]).then_inc(t_hi, 1)
            copy(wt2h, wt2).then_inc(t_hi, 1)
            eng.wait_ge(tower_in, 3)
            for hb in range(2):
                if hb == 0:
                    eng.wait_ge(summed, 4 * TILES)
                    eng.wait_ge(x2_kept, TILES)
                else:
                    eng.wait_ge(l1_made, N1)
                    eng.wait_ge(t_lo, 5)
                cols = slice(hb * HB, (hb + 1) * HB)
                copy(dTh, dT[:, cols]).then_inc(t_hi, 1)
                copy(zfh[:, :, :], zf[:, :, cols]).then_inc(t_hi, 1)
                for a in range(N1):
                    eng.wait_ge(l1_made, N1 * hb + a + 1)
                    wait(eng, l1_lo, N1 * (hb - 1) + a + 1)
                    eng.activation(h1[:, a, :], R[a // 2][:, a % 2, :], ACT.Relu, bias=vec[:, a:a + 1])\
                       .then_inc(l1_kept, 1)
                for a in range(N2):
                    eng.wait_ge(l2_made, N2 * hb + a + 1)
                    wait(eng, y_made, hb)
                    eng.activation(h2[:, a, :], (U0, U1)[a][:, :], ACT.Relu, bias=vec[:, N1 + a:N1 + a + 1])\
                       .then_inc(l2_kept, 1)
                eng.wait_ge(y_made, hb + 1)
                copy(ybuf[hb], XO[0:1, :]).then_inc(y_kept, 1)

        @block.vector
        def _(eng):
            eng.memset(eblk[:, :, :, :], 0.0).then_inc(masks_s, 1)
            eng.wait_ge(const_s, 9 + NQ)
            eng.tensor_reduce(half32[:, :], quad[:, :].rearrange("p (a x) -> p x a", x=2), AX.X, ALU.add).then_inc(masks_s, 1)
            eng.tensor_reduce(half16[:, :], oct_[:, :].rearrange("p (a x) -> p x a", x=2), AX.X, ALU.add).then_inc(masks_s, 1)
            eng.wait_ge(masks_s, 3)
            for x in range(2):
                for t in range(SHIFT_TILES + 1):
                    src = (view(ident32[:, NQ * t:NQ * t + 1], [[1, NQ], [1, F]]) if t < SHIFT_TILES else
                           view(ident32[:, 0:1], [[0, NQ], [1, F]]))
                    eng.tensor_scalar(sel[:, t, x, :].rearrange("p (s h) -> p s h", h=F), src,
                                      half32[:, x:x + 1], None, ALU.mult).then_inc(masks_s, 1)
                for r in range(2):
                    dst = sel16[:, r, :].rearrange("p (c x h) -> p c x h", x=2, h=HALF)[:, :, x, :]
                    eng.tensor_scalar(dst, view(ident32[:, HALF * r:HALF * r + 1], [[0, NQ], [1, HALF]]),
                                      half32[:, x:x + 1], None, ALU.mult).then_inc(masks_s, 1)
            eng.wait_ge(w0_loaded, 16 * W0_DMAS)
            for q in range(1, NQ):
                eng.tensor_tensor(w0a[F * q:F * q + F, 0, :], w0a[F * q:F * q + F, 0, :],
                                  w0b[F * q:F * q + F, 0, :], ALU.add).then_inc(masks_s, 1)
            eng.tensor_tensor(w0a[:, 1:, :], w0a[:, 1:, :], w0b[:, 1:, :], ALU.add).then_inc(masks_s, 1)
            done = 3 + 14 + 4
            eng.wait_ge(masks_s, done)
            eng.tensor_copy(w0h[:, :, :], w0a[:, 0:SHIFT_TILES, :]).then_inc(masks_s, 1)
            eng.tensor_copy(w16h[:, :], w0a[:, SHIFT_TILES, :]).then_inc(masks_s, 1)
            eng.wait_ge(masks_s, done + 2)
            eng.tensor_tensor(w0l[:, :, :], w0a[:, 0:SHIFT_TILES, :], w0h[:, :, :].bitcast(F32), ALU.subtract).then_inc(masks_s, 1)
            for q in range(NQ):
                rows = slice(F * q, F * q + F)
                if q % 2:
                    eng.tensor_tensor(w16[rows, :], w0a[rows, SHIFT_TILES, :], w16h[rows, :].bitcast(F32), ALU.subtract).then_inc(masks_s, 1)
                else:
                    eng.tensor_copy(w16[rows, :], w16h[rows, :].bitcast(F32)).then_inc(masks_s, 1)
            eng.wait_ge(masks_s, done + 7)
            for x in range(2):
                eng.tensor_scalar(w16m[:, x, :], w16[:, :], half16[:, x:x + 1], None, ALU.mult).then_inc(masks_s, 1)

            def s_lo(k, sg):
                eng.wait_ge(s_hi_done, SUPERS * k + sg + 1)
                eng.tensor_tensor(S[sg % 2][2 * F:P, :], U0[0:2 * F, :], S[sg % 2][0:2 * F, :].bitcast(F32),
                                  ALU.subtract).then_inc(s_lo_done, 1)

            def body(k, par, uses, first, last):
                for n in range(CHUNKS):
                    if not last:
                        b = n % 2
                        back = (lambda kind: ZS * k + (zpos(n - 2, kind) if n >= 2 else zpos(n - 2 + CHUNKS, kind) - ZS))
                        eng.wait_ge(e4_done, E4S * k + e4pos(n, "E4") + 1)
                        eng.wait_ge(selected, SEL * k + unit(n, "R01") + 1)
                        wait(eng, zh_done, back("23") + 1)
                        wait(eng, zl_done, back("23") + 1)
                        e4b = view(e4[b][:, 0:1], [[0, 2], [1, BANK]])
                        eng.tensor_tensor(z[b][:, 0:2, :], R[unit(n, "R01") % 2][:, :, :], e4b, ALU.mult).then_inc(z_done, 1)
                        eng.wait_ge(selected, SEL * k + unit(n, "R23") + 1)
                        wait(eng, zl3_done, CHUNKS * k + n - 1)
                        eng.tensor_tensor(z[b][:, 2:4, :], R[unit(n, "R23") % 2][:, :, :], e4b, ALU.mult).then_inc(z_done, 1)
                        eng.wait_ge(zh_done, ZS * k + zpos(n, "01") + 1)
                        wait(eng, x1_made, CHUNKS * k + n - 1)
                        eng.tensor_tensor(zl[b][:, 0:2, :], z[b][:, 0:2, :], zh[b][:, 0:2, :].bitcast(F32), ALU.subtract).then_inc(zl_done, 1)
                        if n % 2 == 0:
                            eng.wait_ge(e4_done, E4S * k + e4pos(n, "B16") + 1)
                            wait(eng, zh_done, ZS * k + zpos(n, "16") + 1 - 5)
                            wait(eng, zl_done, ZS * k + zpos(n, "16") + 1 - 5)
                            eng.tensor_tensor(z16[:, :], R[unit(n, "REM") % 2][:, 1, :], b16[:, :], ALU.mult).then_inc(z_done, 1)
                        eng.wait_ge(zh_done, ZS * k + zpos(n, "23") + 1)
                        eng.tensor_tensor(zl[b][:, 2, :], z[b][:, 2, :], zh[b][:, 2, :].bitcast(F32), ALU.subtract).then_inc(zl_done, 1)
                        if n in (0, 2, 4):
                            s_lo(k, n // 2 + 1)
                        if n == CHUNKS - 1 and not (isinstance(k, int) and k == TILES - 1):
                            s_lo(k + 1, 0)
                        if n % 2 == 0:
                            eng.wait_ge(zh_done, ZS * k + zpos(n, "16") + 1)
                            rows = slice(P // 2, P)
                            eng.tensor_tensor(z16p[n // 2 % 2][rows, :], z16[rows, :],
                                              z16p[n // 2 % 2][rows, :].bitcast(F32), ALU.subtract).then_inc(zl_done, 1)
                        if n in E_UNITS:
                            u = E_UNITS[n]
                            eng.wait_ge(e_transposed, EU * k + u + 1)
                            wait(eng, g_made, UNITS * k)
                            wait(eng, eblk_done, MOVES * k)
                            for r in range(NQ):
                                for q in range(NQ):
                                    src = U0[F * r:F * r + F, :].rearrange("p (h g q) -> p g h q", g=GROUPS, q=NQ)
                                    h = F // EU * u + r
                                    eng.tensor_copy(eblk[F * q:F * q + F, :, q, h:h + F // EU - NQ + 1:NQ], src[:, :, :, q])\
                                       .then_inc(eblk_done, 1)
                    if not first and 1 <= n <= 4:
                        eng.wait_ge(x1_kept, CHUNKS * k)
                        lo = F * (n - 1)
                        eng.tensor_reduce(zf[:, 0, bass.ds(P * (k - 1) + lo, F)], x1[1 - par][:, lo:lo + F, :],
                                          AX.X, ALU.add).then_inc(summed, 1)

            s_lo(0, 0)
            tiles(eng, body)

            eng.wait_ge(t_hi, 3)
            eng.tensor_tensor(wt1l, wt1, wt1h.bitcast(F32), ALU.subtract).then_inc(t_lo, 1)
            eng.tensor_tensor(wt1dl, wt1d[:, :], wt1dh.bitcast(F32), ALU.subtract).then_inc(t_lo, 1)
            eng.tensor_tensor(wt2l, wt2, wt2h.bitcast(F32), ALU.subtract).then_inc(t_lo, 1)
            for hb in range(2):
                eng.wait_ge(t_hi, 3 + 2 * hb + 2)
                cols = slice(hb * HB, (hb + 1) * HB)
                eng.tensor_tensor(dTl, dT[:, cols], dTh.bitcast(F32), ALU.subtract).then_inc(t_lo, 1)
                eng.tensor_tensor(zfl[:, :, :], zf[:, :, cols], zfh[:, :, :].bitcast(F32), ALU.subtract).then_inc(t_lo, 1)
                for a in range(N1):
                    eng.wait_ge(l1_kept, N1 * hb + a + 1)
                    wait(eng, l2_made, N2 * hb)
                    eng.tensor_copy(h1h[:, a, :], h1[:, a, :]).then_inc(l1_hi, 1)
                    eng.wait_ge(l1_hi, N1 * hb + a + 1)
                    eng.tensor_tensor(h1l[:, a, :], h1[:, a, :], h1h[:, a, :].bitcast(F32), ALU.subtract).then_inc(l1_lo, 1)

        @block.tensor
        def _(eng):
            eng.wait_ge(const_s, 9 + NQ)

            def s_transposes(k, sg, par):
                if isinstance(k, int) and k == 0 and sg == 0:
                    pass
                elif sg == 0:
                    eng.wait_ge(eblk_done, MOVES * k)
                else:
                    eng.wait_ge(s_lo_done, SUPERS * k + sg)
                if sg == 0:
                    eng.wait_ge(embd_done, k + 1)
                eng.nop(nofuse=True)
                for dq in range(CD):
                    d = 2 * CD * sg + 2 * dq
                    t = eng.transpose(U0[0:2 * F, P * dq:P * dq + P],
                                      embd[par][:, d:d + 2, :].rearrange("p d h -> p (d h)"), ident[:, :])
                t.then_inc(s_transposed, 1)

            def select(k, n, kind, banks):
                u = unit(n, kind)
                src = S[n // 2 % 2][:, :]
                for i, lhsT in enumerate(banks):
                    m = eng.matmul(R[u % 2][:, i, :], lhsT, src, start=True, stop=True)
                m.then_inc(selected, 1)

            def products(k, n, tiles_):
                b = n % 2
                for t in tiles_:
                    eng.matmul(XO[:, :], w0h[:, t, :], zh[b][:, t, :], start=(t == 0), stop=False)
                    eng.matmul(XO[:, :], w0l[:, t, :], zh[b][:, t, :], start=False, stop=False)
                    eng.matmul(XO[:, :], w0h[:, t, :], zl[b][:, t, :], start=False, stop=False)

            def x1_transposes(k, u, par):
                if u:
                    eng.wait_ge(g_kept, UNITS * (k - 1) + u)
                for i in range(GU):
                    g = GU * u + i
                    t = eng.transpose(U1[:, P * i:P * i + P],
                                      x1[1 - par][:, NQ * g:NQ * g + NQ, :].rearrange("p b d -> p (b d)"), ident[:, :])
                t.then_inc(x1_transposed, 1)

            def g_products(k, u):
                eng.wait_ge(x1t_done, UNITS * (k - 1) + u + 1)
                for i in range(GU):
                    m = eng.matmul(U1[:, P * i:P * i + P], x1t[u % 2][:, i, :],
                                   eblk[:, GU * u + i, :, :].rearrange("p q h -> p (q h)"), start=True, stop=True)
                m.then_inc(g_made, 1)

            def body(k, par, uses, first, last):
                top = not first and not last
                for n in range(CHUNKS):
                    units = G_UNITS.get(n, ()) if not first else ()
                    main = None
                    if n == 0 and not first:
                        main = (k - 1, CHUNKS - 1)
                    elif n > 0 and not last:
                        main = (k, n - 1)
                    if not last:
                        if n % 2 == 0:
                            eng.wait_ge(s_lo_done, SUPERS * k + n // 2 + 1)
                            wait(eng, z_done, ZS * k + (zpos(n - 1, "01") + 1 if n else zpos(CHUNKS - 1, "01") + 1 - ZS))
                        else:
                            wait(eng, z_done, ZS * k + zpos(n - 1, "23") + 1)
                        select(k, n, "E4", [sel[:, SHIFT_TILES, n % 2, :]])
                        if n % 2 == 0:
                            wait(eng, z_done, ZS * k + (zpos(n - 1, "23") + 1 if n else 0))
                        else:
                            eng.wait_ge(z_done, ZS * k + zpos(n - 1, "16") + 1)
                        select(k, n, "R01", [sel[:, 0, n % 2, :], sel[:, 1, n % 2, :]])
                    if units:
                        if units[0] == 0:
                            eng.wait_ge(x1_kept, CHUNKS * k)
                            eng.wait_ge(eblk_done, MOVES * k)
                        x1_transposes(k, units[0], par)
                    if main:
                        mk, mn = main
                        eng.wait_ge(zh_done, ZS * mk + zpos(mn, "23") + 1 + (1 if mn % 2 == 0 else 0))
                        eng.wait_ge(zl_done, ZS * mk + zpos(mn, "23") + 1 + (1 if mn % 2 == 0 else 0))
                        wait(eng, x1_kept, CHUNKS * mk + mn)
                        products(mk, mn, (0, 1))
                    if not last:
                        eng.wait_ge(e4_done, E4S * k + e4pos(n, "E4") + 1)
                        select(k, n, "R23", [sel[:, 2, n % 2, :], sel[:, 3, n % 2, :]])
                    if units:
                        g_products(k, units[0])
                    if main:
                        products(mk, mn, (2,))
                        eng.wait_ge(zl3_done, CHUNKS * mk + mn + 1)
                        products(mk, mn, (3,))
                        eng.matmul(XO[:, :], w16m[:, mn % 2, :], z16p[mn // 2 % 2][:, :], start=False, stop=True)\
                           .then_inc(x1_made, 1)
                    if not last and n % 2 == 0:
                        eng.wait_ge(z_done, ZS * k + zpos(n, "01") + 1)
                        select(k, n, "REM", [sel16[:, 0, :], sel16[:, 1, :]])
                    if not last and n in (0, 2, 4):
                        s_transposes(k, n // 2 + 1, par)
                    if not last and n == CHUNKS - 1 and not (isinstance(k, int) and k == TILES - 1):
                        s_transposes(k + 1, 0, 1 - par)
                    if units:
                        x1_transposes(k, units[1], par)
                    if not first and n in X2_FIELDS:
                        if n == 5:
                            eng.wait_ge(g_kept, UNITS * k)
                        for h in X2_FIELDS[n]:
                            m = eng.matmul(WA[:, 0:P], w1s[:, h, :], G[:, h, :], start=(h == 0), stop=(h == F - 1))
                        if n == CHUNKS - 1:
                            m.then_inc(x2_made, 1)
                    if not last and n in E_UNITS:
                        u = E_UNITS[n]
                        if u == 0:
                            eng.wait_ge(s_lo_done, SUPERS * k + SUPERS)
                        else:
                            eng.wait_ge(eblk_done, MOVES * k + u * MOVES // EU)
                        for i in range(NQ):
                            h = F // EU * u + NQ * i
                            t = eng.transpose(U0[:, P * i:P * i + P],
                                              emb[par][:, h:h + NQ, :].rearrange("p h d -> p (h d)"), ident[:, :])
                        t.then_inc(e_transposed, 1)
                    if units:
                        g_products(k, units[1])

            s_transposes(0, 0, 0)
            eng.wait_ge(masks_s, 3 + 14 + 4 + 2 + 5 + 2)
            eng.wait_ge(w1_loaded, 16)
            tiles(eng, body)

            eng.wait_ge(tower_loaded, 16 * TOWER_DMAS)
            eng.wait_ge(x2_kept, TILES)
            NV = N1 + 2 * N2
            eng.transpose(WA[:, 0:NV], vec_in[:, :], ident[0:NV, 0:NV]).then_inc(vec_transposed, 1)
            for t in range(TILES):
                m = eng.transpose(R[0][0:ND, t // 4, P * (t % 4):P * (t % 4) + P], dense_in[:, t, :], ident[:, :])
                if t % 4 == 3:
                    m.then_inc(dense_transposed, 1)
            for hb in range(2):
                eng.wait_ge(t_lo, 3 + 2 * hb + 2)
                eng.wait_ge(tower_in, 3)
                for a in range(N1):
                    wait(eng, l1_kept, N1 * (hb - 1) + a + 1)
                    o = R[a // 2][:, a % 2, :]
                    cols = slice(P * a, P * a + P)
                    for c in range(KT1):
                        eng.matmul(o, wt1h[:, c, cols], zfh[:, c, :], start=(c == 0), stop=False)
                        eng.matmul(o, wt1l[:, c, cols], zfh[:, c, :], start=False, stop=False)
                        eng.matmul(o, wt1h[:, c, cols], zfl[:, c, :], start=False, stop=False)
                    eng.matmul(o, wt1dh[:, cols], dTh, start=False, stop=False)
                    eng.matmul(o, wt1dl[:, cols], dTh, start=False, stop=False)
                    eng.matmul(o, wt1dh[:, cols], dTl, start=False, stop=True).then_inc(l1_made, 1)
                for a in range(N2):
                    o = (U0, U1)[a][:, :]
                    cols = slice(P * a, P * a + P)
                    wait(eng, l2_kept, N2 * (hb - 1) + a + 1)
                    for c in range(N1):
                        eng.wait_ge(l1_lo, N1 * hb + c + 1)
                        eng.matmul(o, wt2h[:, c, cols], h1h[:, c, :], start=(c == 0), stop=False)
                        eng.matmul(o, wt2l[:, c, cols], h1h[:, c, :], start=False, stop=False)
                        m = eng.matmul(o, wt2h[:, c, cols], h1l[:, c, :], start=False, stop=(c == N1 - 1))
                    m.then_inc(l2_made, 1)
                wait(eng, y_kept, hb)
                for a in range(N2):
                    eng.wait_ge(l2_kept, N2 * hb + a + 1)
                    m = eng.matmul(XO[0:1, :], vec[:, N1 + N2 + a:N1 + N2 + a + 1], h2[:, a, :], start=(a == 0), stop=(a == N2 - 1))
                m.then_inc(y_made, 1)


N_TABLES = 32
_INS = (["dense_ctx", "ids"] + [f"tbl_{f}" for f in range(N_TABLES)] +
        ["W_top1", "b_top1", "W_top2", "b_top2", "W_top3", "L0_rec_W0", "L0_rec_W1"])


def kernel(**inputs):
    import numpy as np
    import concourse.bacc as bacc
    from concourse.bass_utils import run_bass_kernel_spmd

    nc = bacc.Bacc("TRN2", target_bir_lowering=False, num_devices=1)
    arrays, aps = {}, {}
    for name in _INS:
        a = np.ascontiguousarray(inputs[name])
        arrays[f"in_{name}"] = a
        aps[name] = nc.dram_tensor(f"in_{name}", a.shape, mybir.dt.from_np(a.dtype), kind="ExternalInput").ap()
    batch = inputs["ids"].shape[0]
    out = nc.dram_tensor("out_y", (batch, 1), F32, kind="ExternalOutput").ap()
    dlrm_cin_tower(nc, aps["dense_ctx"], aps["ids"], [aps[f"tbl_{f}"] for f in range(N_TABLES)],
                   aps["W_top1"], aps["b_top1"], aps["W_top2"], aps["b_top2"], aps["W_top3"],
                   aps["L0_rec_W0"], aps["L0_rec_W1"], out)
    r = run_bass_kernel_spmd(nc, [arrays], core_ids=[0])
    return r.results[0]["out_y"]
```

```python
import concourse.bass as bass
from concourse import mybir
from contextlib import ExitStack

F32 = mybir.dt.float32
F32R = mybir.dt.float32r
I32 = mybir.dt.int32
ALU = mybir.AluOpType
ACT = mybir.ActivationFunctionType
AX = mybir.AxisListType


def dlrm_cin_tower(nc, dense_ctx, ids, tables, w_top1, b_top1, w_top2, b_top2, w_top3, w0, w1, out):
    B, F = ids.shape
    D = tables[0].shape[1]
    P = 128
    J = w0.shape[1]
    ND = dense_ctx.shape[1]
    H1, H2 = w_top1.shape[1], w_top2.shape[1]
    TILES = B // P
    NQ = P // F
    SHIFT_TILES = 4
    HALF = F // 2
    CD = 4
    CHUNKS = D // CD
    SUPERS = CHUNKS // 2
    BANK = 512
    UNITS = 8
    GROUPS = P // NQ
    GU = GROUPS // UNITS
    KT1 = 2
    N1, N2 = H1 // P, H2 // P
    assert CD * P == BANK and GU * P == BANK and F * NQ == P and D == F and J == P

    ctx = ExitStack()
    with ctx:
        def sb(name, shape, dt=F32):
            return ctx.enter_context(nc.sbuf_tensor(name, shape, dt))

        def ps(name, shape):
            return ctx.enter_context(nc.psum_tensor(name, shape, F32))

        def sem(name):
            return ctx.enter_context(nc.semaphore(name))

        def view(ap, free):
            return bass.AP(ap.tensor, ap.offset, [list(ap.ap[0])] + [list(x) for x in free])

        ident = sb("ident", [P, P])
        ident32 = sb("ident32", [P, 2 * F])
        quad = sb("quad", [P, NQ])
        oct_ = sb("oct", [P, 8])
        half32 = sb("half32", [P, 2])
        half16 = sb("half16", [P, 2])
        sel = sb("sel", [P, 5, 2, P], F32R)
        sel16 = sb("sel16", [P, 2, P], F32R)
        w0h = sb("w0h", [P, SHIFT_TILES, J], F32R)
        w0l = sb("w0l", [P, SHIFT_TILES, J], F32R)
        w16h = sb("w16h", [P, J], F32R)
        w16m = sb("w16m", [P, 2, J], F32R)
        w1s = sb("w1s", [P, F, J])
        idc = [sb(f"idc{i}", [P, F], I32) for i in range(2)]
        emb = [sb(f"emb{i}", [P, F, D]) for i in range(2)]
        embd = [sb(f"embd{i}", [P, D, F]) for i in range(2)]
        S = [sb(f"S{i}", [P, BANK], F32R) for i in range(2)]
        e4 = [sb(f"e4{i}", [P, BANK]) for i in range(2)]
        b16 = sb("b16", [P, BANK])
        z = [sb(f"z{i}", [P, SHIFT_TILES, BANK]) for i in range(2)]
        zh = [sb(f"zh{i}", [P, SHIFT_TILES, BANK], F32R) for i in range(2)]
        zl = [sb(f"zl{i}", [P, SHIFT_TILES, BANK], F32R) for i in range(2)]
        z16 = sb("z16", [P, BANK])
        z16p = [sb(f"z16p{i}", [P, BANK], F32R) for i in range(2)]
        x1 = [sb(f"x1{i}", [P, GROUPS, NQ, D]) for i in range(2)]
        x1t = [sb(f"x1t{i}", [P, GU, P]) for i in range(2)]
        eblk = sb("eblk", [P, GROUPS, NQ, F])
        et = sb("et", [P, F, GROUPS])
        G = sb("G", [P, F, P])
        zf = sb("zf", [P, KT1, B])

        R = [ps(f"R{i}", [P, 2, BANK]) for i in range(2)]
        XO = ps("XO", [P, BANK])
        U0 = ps("U0", [P, BANK])
        U1 = ps("U1", [P, BANK])
        WA = ps("WA", [P, BANK])

        const_s = sem("const_s")
        masks_s = sem("masks_s")
        w0_loaded = sem("w0_loaded")
        w1_loaded = sem("w1_loaded")
        ids_loaded = [sem(f"ids_loaded{i}") for i in range(2)]
        gathered = [sem(f"gathered{i}") for i in range(2)]
        embd_done = sem("embd_done")
        s_transposed = sem("s_transposed")
        s_hi_done = sem("s_hi_done")
        s_lo_done = sem("s_lo_done")
        selected = sem("selected")
        e4_done = sem("e4_done")
        z_done = sem("z_done")
        zh_done = sem("zh_done")
        zl_done = sem("zl_done")
        zl3_done = sem("zl3_done")
        x1_made = sem("x1_made")
        x1_kept = sem("x1_kept")
        summed = sem("summed")
        e_transposed = sem("e_transposed")
        eblk_done = sem("eblk_done")
        x1_transposed = sem("x1_transposed")
        x1t_done = sem("x1t_done")
        g_made = sem("g_made")
        g_kept = sem("g_kept")
        x2_made = sem("x2_made")
        x2_kept = sem("x2_kept")

        def wait(eng, s, value):
            if not (isinstance(value, int) and value <= 0):
                eng.wait_ge(s, value)

        def unit(n, kind):
            return 7 * (n // 2) + ({"E4": 0, "R01": 1, "R23": 2, "REM": 3} if n % 2 == 0 else
                                   {"E4": 4, "R01": 5, "R23": 6})[kind]

        def zpos(n, kind):
            return 5 * (n // 2) + ({"01": 0, "23": 1, "16": 2} if n % 2 == 0 else {"01": 3, "23": 4})[kind]

        def e4pos(n, kind):
            return 3 * (n // 2) + ({"E4": 0, "B16": 1} if n % 2 == 0 else {"E4": 2})[kind]

        SEL, ZS, E4S = 7 * SUPERS, 5 * SUPERS, 3 * SUPERS

        G_UNITS = {n: (2 * (n - 1), 2 * (n - 1) + 1) for n in range(1, 5)}
        SUM_QUARTERS = {1: (0,), 3: (1, 2), 5: (3,)}
        MASK_STEPS = 32
        E_QUARTERS = {5: (0, 1), 6: (2,), 7: (3,)}
        X2_FIELDS = {5: range(0, 10), 6: range(10, 21), 7: range(21, F)}
        GATHERS = {0: 6, 1: 6, 2: 5, 3: 5, 4: 5, 5: 5}

        def tiles(eng, body):
            body(0, 0, 0, True, False)
            with eng.Fori(0, (TILES - 2) // 2) as i:
                body(2 * i + 1, 1, i, False, False)
                body(2 * i + 2, 0, i + 1, False, False)
            body(TILES - 1, 1, (TILES - 1) // 2, False, True)

        raw0, raw1 = (b[:, :, :].rearrange("p t n -> p (t n)") for b in z)
        w0a = raw0[:, 0:5 * J].rearrange("p (t j) -> p t j", j=J)
        w0b = raw0[:, 5 * J:10 * J].rearrange("p (t j) -> p t j", j=J)
        w16 = raw0[:, 10 * J:11 * J]
        wt1d = raw0[0:ND, 11 * J:11 * J + H1]
        wt1 = raw1[:, 0:KT1 * H1].rearrange("p (t n) -> p t n", t=KT1)
        W0_DMAS = 1 + 4 * (4 * SHIFT_TILES - 1) + 2 * (P // HALF)
        TOWER_DMAS = 6

        HB = B // 2
        vec_in = sb("vec_in", [N1 + N2 + N2, P])
        vec = sb("vec", [P, N1 + N2 + N2])
        dense_in = sb("dense_in", [P, TILES, ND])
        wt1h, wt1l = sb("wt1h", [P, KT1, H1], F32R), sb("wt1l", [P, KT1, H1], F32R)
        STACK = [slice(F * i, F * i + ND) for i in range(3)]
        NS = 2 * F + ND
        wt1s = sb("wt1s", [NS, H1], F32R)
        dTs = sb("dTs", [NS, B], F32R)
        wt2 = emb[1][:, :, :].rearrange("p f d -> p (f d)").rearrange("p (t n) -> p t n", t=N1)
        zfh, zfl = zh[0][:, 0:2, :], zl[0][:, 0:2, :]
        wt2h = zh[0][:, 2:4, :].rearrange("p a (b n) -> p (a b) n", n=H2)
        wt2l = zl[0][:, 2:4, :].rearrange("p a (b n) -> p (a b) n", n=H2)
        h1, h1h, h1l = z[0], zh[1], zl[1]
        h2 = z[1][:, 0:N2, :]
        ybuf = [e4[0][0:1, :], e4[1][0:1, :]]

        tower_loaded = sem("tower_loaded")
        wt2_loaded = sem("wt2_loaded")
        vec_transposed = sem("vec_transposed")
        dense_transposed = sem("dense_transposed")
        prep_hi = sem("prep_hi")
        prep_lo = sem("prep_lo")
        t_hi = sem("t_hi")
        t_lo = sem("t_lo")
        l1_made = sem("l1_made")
        l1_kept = sem("l1_kept")
        l1_hi = sem("l1_hi")
        l1_lo = sem("l1_lo")
        l2_made = sem("l2_made")
        l2_kept = sem("l2_kept")
        y_made = sem("y_made")
        y_kept = sem("y_kept")
        y_stored = sem("y_stored")

        block = ctx.enter_context(nc.Block())

        @block.sync
        def _(eng):
            def ids_of(k, par, uses):
                wait(eng, gathered[par], 16 * F * uses)
                eng.dma_start(idc[par][:, :], ids[bass.ds(P * k, P), :]).then_inc(ids_loaded[par], 16)

            ids_of(0, 0, 0)
            ids_of(1, 1, 0)
            for s in range(4 * SHIFT_TILES):
                t, q = s // NQ, s % NQ
                for buf, step, at, wrap in ((w0a, F + 1, s, F), (w0b, F + 1, F * s, F * F)):
                    if s == 0 and buf is w0b:
                        continue
                    n = F - s
                    eng.dma_start(buf[F * q:F * q + n, t, :], w0[at:at + step * (n - 1) + 1:step, :])\
                       .then_inc(w0_loaded, 16)
                    if s:
                        first = at + step * n - wrap
                        eng.dma_start(buf[F * q + n:F * q + F, t, :],
                                      w0[first:first + step * (s - 1) + 1:step, :]).then_inc(w0_loaded, 16)
            for r in range(P // HALF):
                for buf, at in ((w0a, HALF), (w0b, F * HALF)):
                    eng.dma_start(buf[HALF * r:HALF * r + HALF, SHIFT_TILES, :],
                                  w0[at:at + (F + 1) * (HALF - 1) + 1:F + 1, :]).then_inc(w0_loaded, 16)
            eng.dma_start(w1s[:, :, :], w1.rearrange("(h m) j -> m h j", m=P)).then_inc(w1_loaded, 16)
            eng.dma_start(wt1, w_top1[0:KT1 * P, :].rearrange("(t p) n -> p t n", p=P)).then_inc(tower_loaded, 16)
            eng.dma_start(wt1d, w_top1[KT1 * P:KT1 * P + ND, :]).then_inc(tower_loaded, 16)
            eng.dma_start(vec_in[0:N1, :], b_top1.rearrange("(t p) -> t p", p=P)).then_inc(tower_loaded, 16)
            eng.dma_start(vec_in[N1:N1 + N2, :], b_top2.rearrange("(t p) -> t p", p=P)).then_inc(tower_loaded, 16)
            eng.dma_start(vec_in[N1 + N2:, :], w_top3.rearrange("(t p) o -> t (p o)", p=P)).then_inc(tower_loaded, 16)
            eng.dma_start(dense_in[:, :, :], dense_ctx.rearrange("(t p) n -> p t n", p=P)).then_inc(tower_loaded, 16)
            with eng.Fori(1, TILES // 2) as i:
                ids_of(2 * i, 0, i)
                ids_of(2 * i + 1, 1, i)
            eng.wait_ge(e_transposed, TILES)
            eng.wait_ge(embd_done, TILES)
            eng.dma_start(wt2, w_top2.rearrange("(t p) n -> p t n", p=P)).then_inc(wt2_loaded, 16)
            for hb in range(2):
                eng.wait_ge(y_kept, hb + 1)
                eng.dma_start(out[hb * HB:(hb + 1) * HB, :].rearrange("b o -> o b"), ybuf[hb]).then_inc(y_stored, 16)
            eng.wait_ge(y_stored, 32)

        @block.gpsimd
        def _(eng):
            eng.memset(ident[:, :], 0.0).then_inc(const_s, 1)
            eng.memset(ident32[:, :], 0.0).then_inc(const_s, 1)
            eng.memset(quad[:, :], 1.0).then_inc(const_s, 1)
            eng.memset(oct_[:, :], 1.0).then_inc(const_s, 1)
            eng.wait_ge(const_s, 4)
            eng.affine_select(out=ident[:, :], in_=ident[:, :], compare_op=ALU.not_equal, fill=1.0,
                              base=0, pattern=[[-1, P]], channel_multiplier=1).then_inc(const_s, 1)
            eng.affine_select(out=quad[:, :], in_=quad[:, :], compare_op=ALU.is_ge, fill=0.0,
                              base=0, pattern=[[-F, NQ]], channel_multiplier=1).then_inc(const_s, 1)
            eng.affine_select(out=oct_[:, :], in_=oct_[:, :], compare_op=ALU.is_ge, fill=0.0,
                              base=0, pattern=[[-HALF, 8]], channel_multiplier=1).then_inc(const_s, 1)
            eng.wait_ge(const_s, 7)
            eng.affine_select(out=quad[:, :], in_=quad[:, :], compare_op=ALU.is_ge, fill=0.0,
                              base=F - 1, pattern=[[F, NQ]], channel_multiplier=-1).then_inc(const_s, 1)
            eng.affine_select(out=oct_[:, :], in_=oct_[:, :], compare_op=ALU.is_ge, fill=0.0,
                              base=HALF - 1, pattern=[[HALF, 8]], channel_multiplier=-1).then_inc(const_s, 1)
            for a in range(NQ):
                eng.wait_ge(const_s, 9 + a)
                eng.affine_select(out=ident32[:, :].rearrange("p (c h) -> p c h", h=F),
                                  in_=ident32[:, :].rearrange("p (c h) -> p c h", h=F),
                                  compare_op=ALU.not_equal, fill=1.0, base=-F * a,
                                  pattern=[[0, 2], [-1, F]], channel_multiplier=1).then_inc(const_s, 1)

            def gather(k, par, uses, fields):
                for f in fields:
                    eng.indirect_dma_start(emb[par][:, f, :], None, tables[f],
                                           bass.IndirectOffsetOnAxis(idc[par][:, f:f + 1], 0))\
                       .then_inc(gathered[par], 16)

            eng.wait_ge(ids_loaded[0], 16)
            gather(0, 0, 0, range(F))

            def body(k, par, uses, first, last):
                f = 0
                for n in range(CHUNKS):
                    if not last and n in GATHERS:
                        if n == 0:
                            eng.wait_ge(ids_loaded[1 - par], 16 * (uses + par + 1))
                            wait(eng, e_transposed, k)
                            eng.nop(nofuse=True)
                        gather(k + 1, 1 - par, 0, range(f, f + GATHERS[n]))
                        f += GATHERS[n]
                    eng.wait_ge(zh_done, ZS * k + zpos(n, "23") + 1)
                    wait(eng, x1_made, CHUNKS * k + n - 1)
                    eng.tensor_tensor(zl[n % 2][:, 3, :], z[n % 2][:, 3, :], zh[n % 2][:, 3, :].bitcast(F32),
                                      ALU.subtract).then_inc(zl3_done, 1)

            tiles(eng, body)

        @block.scalar
        def _(eng):
            def copy(dst, src):
                return eng.activation(dst, src, ACT.Copy)

            def by_d(k, par, uses):
                eng.wait_ge(gathered[par], 16 * F * (uses + 1))
                wait(eng, s_transposed, SUPERS * (k - 1))
                copy(embd[par][:, :, :], emb[par][:, :, :].rearrange("p f d -> p d f")).then_inc(embd_done, 1)

            def s_hi(k, sg):
                eng.wait_ge(s_transposed, SUPERS * k + sg + 1)
                wait(eng, selected, SEL * k + 7 * (sg - 1))
                copy(S[sg % 2][0:2 * F, :], U0[0:2 * F, :]).then_inc(s_hi_done, 1)

            def x1t_copy(tile, u):
                eng.wait_ge(x1_transposed, UNITS * tile + u + 1)
                if u > 1:
                    eng.wait_ge(g_made, UNITS * tile + u - 1)
                copy(x1t[u % 2][:, :, :], U0[:, :]).then_inc(x1t_done, 1)

            def g_copy(tile, u):
                eng.wait_ge(g_made, UNITS * tile + u + 1)
                copy(G[:, :, :].rearrange("p h (q g) -> p h q g", q=NQ)[:, :, :, GU * u:GU * u + GU],
                     U1[:, :].rearrange("p (g q h) -> p h q g", g=GU, q=NQ)).then_inc(g_kept, 1)

            def x1_copy(tile, m, par):
                eng.wait_ge(x1_made, CHUNKS * tile + m + 1)
                d = 2 * CD * (m // 2) + m % 2
                copy(x1[par][:, :, :, d:d + 2 * CD - 1:2].rearrange("p g q d -> p q g d"),
                     XO[:, :].rearrange("p (d q g) -> p q g d", d=CD, q=NQ)).then_inc(x1_kept, 1)

            def x2_copy(tile):
                eng.wait_ge(x2_made, tile + 1)
                copy(zf[:, 1, bass.ds(P * tile, P)], WA[:, 0:P]).then_inc(x2_kept, 1)

            def body(k, par, uses, first, last):
                for n in range(CHUNKS):
                    units = G_UNITS.get(n, ()) if not first else ()
                    eng.wait_ge(selected, SEL * k + unit(n, "E4") + 1)
                    wait(eng, z_done, ZS * k + (zpos(n - 2, "23") + 1 if n >= 2 else zpos(n - 2 + CHUNKS, "23") + 1 - ZS))
                    copy(e4[n % 2][:, :], R[unit(n, "E4") % 2][:, 0, :]).then_inc(e4_done, 1)
                    if units:
                        x1t_copy(k - 1, units[0])
                    eng.wait_ge(z_done, ZS * k + zpos(n, "01") + 1)
                    wait(eng, x1_made, CHUNKS * k + n - 1)
                    copy(zh[n % 2][:, 0:2, :], z[n % 2][:, 0:2, :]).then_inc(zh_done, 1)
                    if n % 2 == 0:
                        eng.wait_ge(selected, SEL * k + unit(n, "REM") + 1)
                        wait(eng, z_done, ZS * k + zpos(n, "16") + 1 - 5)
                        copy(b16[:, :], R[unit(n, "REM") % 2][:, 0, :]).then_inc(e4_done, 1)
                    if units:
                        g_copy(k - 1, units[0])
                    eng.wait_ge(z_done, ZS * k + zpos(n, "23") + 1)
                    copy(zh[n % 2][:, 2:4, :], z[n % 2][:, 2:4, :]).then_inc(zh_done, 1)
                    if units:
                        x1t_copy(k - 1, units[1])
                    if n % 2 == 0:
                        eng.wait_ge(z_done, ZS * k + zpos(n, "16") + 1)
                        wait(eng, x1_made, CHUNKS * k + n - 2)
                        copy(z16p[n // 2 % 2][:, :], z16[:, :]).then_inc(zh_done, 1)
                    if n:
                        x1_copy(k, n - 1, par)
                    elif not first:
                        x1_copy(k - 1, CHUNKS - 1, 1 - par)
                    if units:
                        g_copy(k - 1, units[1])
                    if n in (0, 2, 4):
                        s_hi(k, n // 2 + 1)
                    if n == CHUNKS - 2 and not last:
                        by_d(k + 1, 1 - par, uses + par)
                    if n == CHUNKS - 1 and not last:
                        s_hi(k + 1, 0)
                    if n == CHUNKS - 1 and not first:
                        x2_copy(k - 1)

            eng.wait_ge(vec_transposed, 1)
            copy(vec[:, :], WA[:, 0:N1 + 2 * N2]).then_inc(prep_hi, 1)
            eng.wait_ge(tower_loaded, 16 * TOWER_DMAS)
            copy(wt1h[:, :, :], wt1).then_inc(prep_hi, 1)
            eng.wait_ge(masks_s, 3)
            for rows in (STACK[0], STACK[2]):
                copy(wt1s[rows, :], wt1d).then_inc(prep_hi, 1)
            for hb in range(2):
                eng.wait_ge(dense_transposed, hb + 1)
                for rows in STACK[0:2]:
                    copy(dTs[rows, hb * HB:(hb + 1) * HB], R[0][0:ND, hb, :]).then_inc(prep_hi, 1)

            by_d(0, 0, 0)
            s_hi(0, 0)
            tiles(eng, body)

            def features(hb):
                copy(zfh, zf[:, :, hb * HB:(hb + 1) * HB]).then_inc(t_hi, 1)

            def hidden1(hb, a):
                eng.wait_ge(l1_made, N1 * hb + a + 1)
                wait(eng, l1_lo, N1 * (hb - 1) + a + 1)
                eng.activation(h1[:, a, :], R[1 - a // 2][:, a % 2, :], ACT.Relu, bias=vec[:, a:a + 1])\
                   .then_inc(l1_kept, 1)

            def hidden2(hb, a):
                eng.wait_ge(l2_made, N2 * hb + a + 1)
                wait(eng, y_made, hb)
                eng.activation(h2[:, a, :], (U0, U1)[a][:, :], ACT.Relu, bias=vec[:, N1 + a:N1 + a + 1])\
                   .then_inc(l2_kept, 1)

            def result(hb):
                eng.wait_ge(y_made, hb + 1)
                copy(ybuf[hb], XO[0:1, :]).then_inc(y_kept, 1)

            t = TILES - 1
            eng.wait_ge(x1_made, CHUNKS * TILES - 1)
            eng.wait_ge(summed, NQ * (TILES // 2))
            eng.wait_ge(x2_kept, TILES // 2)
            features(0)
            x1_copy(t, CHUNKS - 1, t % 2)
            x1t_copy(t, 0)
            for u in range(UNITS):
                g_copy(t, u)
                if u + 1 < UNITS:
                    x1t_copy(t, u + 1)
                if u == 0:
                    eng.wait_ge(wt2_loaded, 16)
                    copy(wt2h, wt2).then_inc(t_hi, 1)
                if u % 2:
                    hidden1(0, u // 2)
            x2_copy(t)
            eng.wait_ge(summed, NQ * TILES)
            eng.wait_ge(x2_kept, TILES)
            eng.wait_ge(t_lo, 1)
            features(1)
            for a in range(N2):
                hidden2(0, a)
            for a in range(N1):
                hidden1(1, a)
            result(0)
            for a in range(N2):
                hidden2(1, a)
            result(1)

        @block.vector
        def _(eng):
            eng.memset(eblk[:, :, :, :], 0.0).then_inc(masks_s, 1)
            eng.memset(wt1s[:, :].bitcast(F32), 0.0).then_inc(masks_s, 1)
            eng.memset(dTs[:, :].bitcast(F32), 0.0).then_inc(masks_s, 1)
            eng.wait_ge(const_s, 9 + NQ)
            eng.tensor_reduce(half32[:, :], quad[:, :].rearrange("p (a x) -> p x a", x=2), AX.X, ALU.add).then_inc(masks_s, 1)
            eng.tensor_reduce(half16[:, :], oct_[:, :].rearrange("p (a x) -> p x a", x=2), AX.X, ALU.add).then_inc(masks_s, 1)
            eng.wait_ge(masks_s, 5)
            for x in range(2):
                for t in range(SHIFT_TILES + 1):
                    src = (view(ident32[:, NQ * t:NQ * t + 1], [[1, NQ], [1, F]]) if t < SHIFT_TILES else
                           view(ident32[:, 0:1], [[0, NQ], [1, F]]))
                    eng.tensor_scalar(sel[:, t, x, :].rearrange("p (s h) -> p s h", h=F), src,
                                      half32[:, x:x + 1], None, ALU.mult).then_inc(masks_s, 1)
                for r in range(2):
                    dst = sel16[:, r, :].rearrange("p (c x h) -> p c x h", x=2, h=HALF)[:, :, x, :]
                    eng.tensor_scalar(dst, view(ident32[:, HALF * r:HALF * r + 1], [[0, NQ], [1, HALF]]),
                                      half32[:, x:x + 1], None, ALU.mult).then_inc(masks_s, 1)
            eng.wait_ge(w0_loaded, 16 * W0_DMAS)
            for q in range(1, NQ):
                eng.tensor_tensor(w0a[F * q:F * q + F, 0, :], w0a[F * q:F * q + F, 0, :],
                                  w0b[F * q:F * q + F, 0, :], ALU.add).then_inc(masks_s, 1)
            eng.tensor_tensor(w0a[:, 1:, :], w0a[:, 1:, :], w0b[:, 1:, :], ALU.add).then_inc(masks_s, 1)
            done = 5 + 14 + 4
            eng.wait_ge(masks_s, done)
            eng.tensor_copy(w0h[:, :, :], w0a[:, 0:SHIFT_TILES, :]).then_inc(masks_s, 1)
            eng.tensor_copy(w16h[:, :], w0a[:, SHIFT_TILES, :]).then_inc(masks_s, 1)
            eng.wait_ge(masks_s, done + 2)
            eng.tensor_tensor(w0l[:, :, :], w0a[:, 0:SHIFT_TILES, :], w0h[:, :, :].bitcast(F32), ALU.subtract).then_inc(masks_s, 1)
            for q in range(NQ):
                rows = slice(F * q, F * q + F)
                if q % 2:
                    eng.tensor_tensor(w16[rows, :], w0a[rows, SHIFT_TILES, :], w16h[rows, :].bitcast(F32), ALU.subtract).then_inc(masks_s, 1)
                else:
                    eng.tensor_copy(w16[rows, :], w16h[rows, :].bitcast(F32)).then_inc(masks_s, 1)
            eng.wait_ge(masks_s, done + 7)
            assert done + 7 + 2 == MASK_STEPS
            for x in range(2):
                eng.tensor_scalar(w16m[:, x, :], w16[:, :], half16[:, x:x + 1], None, ALU.mult).then_inc(masks_s, 1)

            def s_lo(k, sg):
                eng.wait_ge(s_hi_done, SUPERS * k + sg + 1)
                eng.tensor_tensor(S[sg % 2][2 * F:P, :], U0[0:2 * F, :], S[sg % 2][0:2 * F, :].bitcast(F32),
                                  ALU.subtract).then_inc(s_lo_done, 1)

            def sum_d(tile, q, par):
                eng.tensor_reduce(zf[:, 0, bass.ds(P * tile + F * q, F)], x1[par][:, :, q, :], AX.X, ALU.add)\
                   .then_inc(summed, 1)

            def body(k, par, uses, first, last):
                for n in range(CHUNKS):
                    b = n % 2
                    eng.wait_ge(e4_done, E4S * k + e4pos(n, "E4") + 1)
                    eng.wait_ge(selected, SEL * k + unit(n, "R01") + 1)
                    back = ZS * k + (zpos(n - 2, "23") if n >= 2 else zpos(n - 2 + CHUNKS, "23") - ZS) + 1
                    wait(eng, zh_done, back)
                    wait(eng, zl_done, back)
                    e4b = view(e4[b][:, 0:1], [[0, 2], [1, BANK]])
                    eng.tensor_tensor(z[b][:, 0:2, :], R[unit(n, "R01") % 2][:, :, :], e4b, ALU.mult).then_inc(z_done, 1)
                    eng.wait_ge(selected, SEL * k + unit(n, "R23") + 1)
                    wait(eng, zl3_done, CHUNKS * k + n - 1)
                    eng.tensor_tensor(z[b][:, 2:4, :], R[unit(n, "R23") % 2][:, :, :], e4b, ALU.mult).then_inc(z_done, 1)
                    if n % 2 == 0:
                        eng.wait_ge(e4_done, E4S * k + e4pos(n, "B16") + 1)
                        wait(eng, zh_done, ZS * k + zpos(n, "16") + 1 - 5)
                        wait(eng, zl_done, ZS * k + zpos(n, "16") + 1 - 5)
                        eng.tensor_tensor(z16[:, :], R[unit(n, "REM") % 2][:, 1, :], b16[:, :], ALU.mult).then_inc(z_done, 1)
                    eng.wait_ge(zh_done, ZS * k + zpos(n, "01") + 1)
                    wait(eng, x1_made, CHUNKS * k + n - 1)
                    eng.tensor_tensor(zl[b][:, 0:2, :], z[b][:, 0:2, :], zh[b][:, 0:2, :].bitcast(F32), ALU.subtract).then_inc(zl_done, 1)
                    eng.wait_ge(zh_done, ZS * k + zpos(n, "23") + 1)
                    eng.tensor_tensor(zl[b][:, 2, :], z[b][:, 2, :], zh[b][:, 2, :].bitcast(F32), ALU.subtract).then_inc(zl_done, 1)
                    if n % 2 == 0:
                        eng.wait_ge(zh_done, ZS * k + zpos(n, "16") + 1)
                        rows = slice(P // 2, P)
                        eng.tensor_tensor(z16p[n // 2 % 2][rows, :], z16[rows, :],
                                          z16p[n // 2 % 2][rows, :].bitcast(F32), ALU.subtract).then_inc(zl_done, 1)
                    if n == 4:
                        eng.wait_ge(gathered[par], 16 * F * (uses + 1))
                        wait(eng, eblk_done, NQ * k)
                        eng.transpose(et[:, :, :].rearrange("p h g -> p (h g)"),
                                      emb[par][:, :, :].rearrange("p h d -> p (h d)")).then_inc(e_transposed, 1)
                    for q in E_QUARTERS.get(n, ()):
                        eng.wait_ge(e_transposed, k + 1)
                        wait(eng, g_made, UNITS * k)
                        wait(eng, eblk_done, NQ * k)
                        rows = slice(F * q, F * q + F)
                        eng.tensor_copy(eblk[rows, :, q, :], et[rows, :, :].rearrange("p h g -> p g h"))\
                           .then_inc(eblk_done, 1)
                    if not first and n in SUM_QUARTERS:
                        eng.wait_ge(x1_kept, CHUNKS * k)
                        for q in SUM_QUARTERS[n]:
                            sum_d(k - 1, q, 1 - par)
                    if n in (0, 2, 4):
                        s_lo(k, n // 2 + 1)
                    if n == CHUNKS - 1 and not last:
                        s_lo(k + 1, 0)

            eng.wait_ge(prep_hi, 2 + 2 * 3)
            eng.tensor_tensor(wt1l[:, :, :], wt1, wt1h[:, :, :].bitcast(F32), ALU.subtract).then_inc(prep_lo, 1)
            eng.tensor_tensor(wt1s[STACK[1], :], wt1d, wt1s[0:ND, :].bitcast(F32), ALU.subtract).then_inc(prep_lo, 1)
            for hb in range(2):
                cols = slice(hb * HB, (hb + 1) * HB)
                eng.tensor_tensor(dTs[STACK[2], cols], R[0][0:ND, hb, :], dTs[0:ND, cols].bitcast(F32), ALU.subtract).then_inc(prep_lo, 1)
            eng.wait_ge(prep_lo, 4)
            eng.wait_ge(masks_s, MASK_STEPS)

            s_lo(0, 0)
            tiles(eng, body)

            def features(hb):
                eng.tensor_tensor(zfl, zf[:, :, hb * HB:(hb + 1) * HB], zfh.bitcast(F32), ALU.subtract).then_inc(t_lo, 1)

            def hidden1(hb, a):
                eng.wait_ge(l1_kept, N1 * hb + a + 1)
                wait(eng, l2_made, N2 * hb)
                eng.tensor_copy(h1h[:, a, :], h1[:, a, :]).then_inc(l1_hi, 1)
                eng.wait_ge(l1_hi, N1 * hb + a + 1)
                eng.tensor_tensor(h1l[:, a, :], h1[:, a, :], h1h[:, a, :].bitcast(F32), ALU.subtract).then_inc(l1_lo, 1)

            eng.wait_ge(t_hi, 1)
            features(0)
            eng.wait_ge(x1_kept, CHUNKS * TILES)
            for q in range(NQ):
                sum_d(TILES - 1, q, (TILES - 1) % 2)
            eng.wait_ge(t_hi, 2)
            eng.tensor_tensor(wt2l, wt2, wt2h.bitcast(F32), ALU.subtract).then_inc(t_lo, 1)
            for a in range(N1):
                hidden1(0, a)
            eng.wait_ge(t_hi, 3)
            eng.wait_ge(l1_made, N1)
            features(1)
            for a in range(N1):
                hidden1(1, a)

        @block.tensor
        def _(eng):
            eng.wait_ge(const_s, 9 + NQ)

            def s_transposes(k, sg, par, first):
                if sg >= 2 and not first:
                    eng.wait_ge(x1t_done, UNITS * (k - 1) + {2: 4, 3: UNITS}[sg])
                elif sg or not isinstance(k, int) or k:
                    eng.wait_ge(s_lo_done, SUPERS * k + sg)
                if sg == 0:
                    eng.wait_ge(embd_done, k + 1)
                eng.nop(nofuse=True)
                for dq in range(CD):
                    d = 2 * CD * sg + 2 * dq
                    t = eng.transpose(U0[0:2 * F, P * dq:P * dq + P],
                                      embd[par][:, d:d + 2, :].rearrange("p d h -> p (d h)"), ident[:, :])
                t.then_inc(s_transposed, 1)

            def select(k, n, kind, banks):
                u = unit(n, kind)
                src = S[n // 2 % 2][:, :]
                for i, lhsT in enumerate(banks):
                    m = eng.matmul(R[u % 2][:, i, :], lhsT, src, start=True, stop=True)
                m.then_inc(selected, 1)

            def products(k, n, t):
                b = n % 2
                eng.matmul(XO[:, :], w0h[:, t, :], zh[b][:, t, :], start=(t == 0), stop=False)
                eng.matmul(XO[:, :], w0l[:, t, :], zh[b][:, t, :], start=False, stop=False)
                m = eng.matmul(XO[:, :], w0h[:, t, :], zl[b][:, t, :], start=False, stop=(t == SHIFT_TILES - 1))
                return m

            def products_a(k, n):
                eng.wait_ge(zh_done, ZS * k + zpos(n, "01") + 1)
                eng.wait_ge(zl_done, ZS * k + zpos(n, "01") + 1)
                wait(eng, x1_kept, CHUNKS * k + n)
                products(k, n, 0)
                products(k, n, 1)

            def products_b(k, n):
                rem = 1 if n % 2 == 0 else 0
                eng.wait_ge(zh_done, ZS * k + zpos(n, "23") + 1 + rem)
                eng.wait_ge(zl_done, ZS * k + zpos(n, "23") + 1 + rem)
                products(k, n, 2)
                eng.matmul(XO[:, :], w16m[:, n % 2, :], z16p[n // 2 % 2][:, :], start=False, stop=False)
                eng.wait_ge(zl3_done, CHUNKS * k + n + 1)
                products(k, n, 3).then_inc(x1_made, 1)

            def x1_transposes(tile, u, par):
                for i in range(GU):
                    t = eng.transpose(U0[:, P * i:P * i + P],
                                      x1[par][:, GU * u + i, :, :].rearrange("p q d -> p (q d)"), ident[:, :])
                t.then_inc(x1_transposed, 1)

            def g_products(tile, u):
                eng.wait_ge(x1t_done, UNITS * tile + u + 1)
                if u:
                    eng.wait_ge(g_kept, UNITS * tile + u)
                for i in range(GU):
                    m = eng.matmul(U1[:, P * i:P * i + P], x1t[u % 2][:, i, :],
                                   eblk[:, GU * u + i, :, :].rearrange("p q h -> p (q h)"), start=True, stop=True)
                m.then_inc(g_made, 1)

            def x2_products(fields):
                for h in fields:
                    m = eng.matmul(WA[:, 0:P], w1s[:, h, :], G[:, h, :], start=(h == 0), stop=(h == F - 1))
                return m

            def body(k, par, uses, first, last):
                for n in range(CHUNKS):
                    units = G_UNITS.get(n, ()) if not first else ()
                    main = (k, n - 1) if n else None if first else (k - 1, CHUNKS - 1)
                    if n % 2 == 0:
                        eng.wait_ge(s_lo_done, SUPERS * k + n // 2 + 1)
                        wait(eng, z_done, ZS * k + (zpos(n - 1, "01") + 1 if n else zpos(CHUNKS - 1, "01") + 1 - ZS))
                    else:
                        wait(eng, z_done, ZS * k + zpos(n - 1, "23") + 1)
                    select(k, n, "E4", [sel[:, SHIFT_TILES, n % 2, :]])
                    if n % 2 == 0:
                        wait(eng, z_done, ZS * k + (zpos(n - 1, "23") + 1 if n else 0))
                    else:
                        eng.wait_ge(z_done, ZS * k + zpos(n - 1, "16") + 1)
                    select(k, n, "R01", [sel[:, 0, n % 2, :], sel[:, 1, n % 2, :]])
                    if units:
                        u = units[0]
                        if u == 0:
                            eng.wait_ge(x1_kept, CHUNKS * k)
                            eng.wait_ge(eblk_done, NQ * k)
                            eng.wait_ge(s_lo_done, SUPERS * k + 2)
                        elif u == 4:
                            eng.wait_ge(s_lo_done, SUPERS * k + 3)
                        else:
                            eng.wait_ge(x1t_done, UNITS * (k - 1) + u)
                        x1_transposes(k - 1, u, 1 - par)
                    eng.wait_ge(e4_done, E4S * k + e4pos(n, "E4") + 1)
                    select(k, n, "R23", [sel[:, 2, n % 2, :], sel[:, 3, n % 2, :]])
                    if main:
                        products_a(*main)
                    if n % 2 == 0:
                        eng.wait_ge(z_done, ZS * k + zpos(n, "01") + 1)
                        select(k, n, "REM", [sel16[:, 0, :], sel16[:, 1, :]])
                    if units:
                        g_products(k - 1, units[0])
                        eng.wait_ge(x1t_done, UNITS * (k - 1) + units[1])
                        x1_transposes(k - 1, units[1], 1 - par)
                    if main:
                        products_b(*main)
                    if units:
                        g_products(k - 1, units[1])
                    if n in (0, 2, 4):
                        s_transposes(k, n // 2 + 1, par, first)
                    if n == CHUNKS - 1 and not last:
                        s_transposes(k + 1, 0, 1 - par, first)
                    if not first and n in X2_FIELDS:
                        if n == 5:
                            eng.wait_ge(g_kept, UNITS * k)
                        m = x2_products(X2_FIELDS[n])
                        if n == CHUNKS - 1:
                            m.then_inc(x2_made, 1)

            eng.wait_ge(tower_loaded, 16 * TOWER_DMAS)
            NV = N1 + 2 * N2
            eng.transpose(WA[:, 0:NV], vec_in[:, :], ident[0:NV, 0:NV]).then_inc(vec_transposed, 1)
            for t in range(TILES):
                m = eng.transpose(R[0][0:ND, t // 4, P * (t % 4):P * (t % 4) + P], dense_in[:, t, :], ident[:, :])
                if t % 4 == 3:
                    m.then_inc(dense_transposed, 1)
            s_transposes(0, 0, 0, True)
            eng.wait_ge(masks_s, MASK_STEPS)
            eng.wait_ge(prep_lo, 4)
            eng.wait_ge(w1_loaded, 16)
            tiles(eng, body)

            def hidden1(hb, a):
                cols, half = slice(P * a, P * a + P), slice(hb * HB, (hb + 1) * HB)
                pairs = []
                for c in range(KT1):
                    pairs += [(wt1h[:, c, cols], zfh[:, c, :]), (wt1l[:, c, cols], zfh[:, c, :]),
                              (wt1h[:, c, cols], zfl[:, c, :])]
                return pairs + [(wt1s[:, cols], dTs[:, half])]

            def hidden1_products(hb, a, part):
                pairs = hidden1(hb, a)
                for i in part:
                    m = eng.matmul(R[1 - a // 2][:, a % 2, :], *pairs[i], start=(i == 0), stop=(i == len(pairs) - 1))
                    if i == len(pairs) - 1:
                        m.then_inc(l1_made, 1)

            def hidden2_products(hb):
                for a in range(N2):
                    o = (U0, U1)[a][:, :]
                    cols = slice(P * a, P * a + P)
                    wait(eng, l2_kept, N2 * (hb - 1) + a + 1)
                    eng.wait_ge(t_lo, 2)
                    for c in range(N1):
                        eng.wait_ge(l1_lo, N1 * hb + c + 1)
                        eng.matmul(o, wt2h[:, c, cols], h1h[:, c, :], start=(c == 0), stop=False)
                        eng.matmul(o, wt2l[:, c, cols], h1h[:, c, :], start=False, stop=False)
                        m = eng.matmul(o, wt2h[:, c, cols], h1l[:, c, :], start=False, stop=(c == N1 - 1))
                    m.then_inc(l2_made, 1)

            def result(hb):
                wait(eng, y_kept, hb)
                for a in range(N2):
                    eng.wait_ge(l2_kept, N2 * hb + a + 1)
                    m = eng.matmul(XO[0:1, :], vec[:, N1 + N2 + a:N1 + N2 + a + 1], h2[:, a, :], start=(a == 0), stop=(a == N2 - 1))
                m.then_inc(y_made, 1)

            t = TILES - 1
            products_a(t, CHUNKS - 1)
            products_b(t, CHUNKS - 1)
            eng.wait_ge(x1_kept, CHUNKS * TILES)
            eng.wait_ge(eblk_done, NQ * TILES)
            x1_transposes(t, 0, t % 2)
            eng.wait_ge(t_lo, 1)
            eng.wait_ge(z_done, ZS * TILES)
            for u in range(UNITS):
                hidden1_products(0, u // 2, range(4) if u % 2 == 0 else range(4, 7))
                g_products(t, u)
                if u + 1 < UNITS:
                    eng.wait_ge(x1t_done, UNITS * t + u + 1)
                    x1_transposes(t, u + 1, t % 2)
            eng.wait_ge(g_kept, UNITS * TILES)
            x2_products(range(F)).then_inc(x2_made, 1)
            hidden2_products(0)
            eng.wait_ge(t_lo, 3)
            for a in range(N1):
                eng.wait_ge(l1_kept, a + 1)
                hidden1_products(1, a, range(7))
            result(0)
            hidden2_products(1)
            result(1)


N_TABLES = 32
_INS = (["dense_ctx", "ids"] + [f"tbl_{f}" for f in range(N_TABLES)] +
        ["W_top1", "b_top1", "W_top2", "b_top2", "W_top3", "L0_rec_W0", "L0_rec_W1"])


def kernel(**inputs):
    import numpy as np
    import concourse.bacc as bacc
    from concourse.bass_utils import run_bass_kernel_spmd

    nc = bacc.Bacc("TRN2", target_bir_lowering=False, num_devices=1)
    arrays, aps = {}, {}
    for name in _INS:
        a = np.ascontiguousarray(inputs[name])
        arrays[f"in_{name}"] = a
        aps[name] = nc.dram_tensor(f"in_{name}", a.shape, mybir.dt.from_np(a.dtype), kind="ExternalInput").ap()
    batch = inputs["ids"].shape[0]
    out = nc.dram_tensor("out_y", (batch, 1), F32, kind="ExternalOutput").ap()
    dlrm_cin_tower(nc, aps["dense_ctx"], aps["ids"], [aps[f"tbl_{f}"] for f in range(N_TABLES)],
                   aps["W_top1"], aps["b_top1"], aps["W_top2"], aps["b_top2"], aps["W_top3"],
                   aps["L0_rec_W0"], aps["L0_rec_W1"], out)
    r = run_bass_kernel_spmd(nc, [arrays], core_ids=[0])
    return r.results[0]["out_y"]
```

```python
import concourse.bass as bass
from concourse import mybir
from contextlib import ExitStack

F32 = mybir.dt.float32
F32R = mybir.dt.float32r
I32 = mybir.dt.int32
ALU = mybir.AluOpType
ACT = mybir.ActivationFunctionType
AX = mybir.AxisListType


def dlrm_cin_tower(nc, dense_ctx, ids, tables, w_top1, b_top1, w_top2, b_top2, w_top3, w0, w1, out):
    B, F = ids.shape
    D = tables[0].shape[1]
    P = 128
    J = w0.shape[1]
    ND = dense_ctx.shape[1]
    H1, H2 = w_top1.shape[1], w_top2.shape[1]
    TILES = B // P
    NQ = P // F
    SHIFT_TILES = 4
    HALF = F // 2
    CD = 4
    CHUNKS = D // CD
    SUPERS = CHUNKS // 2
    BANK = 512
    UNITS = 8
    GROUPS = P // NQ
    GU = GROUPS // UNITS
    KT1 = 2
    N1, N2 = H1 // P, H2 // P
    assert CD * P == BANK and GU * P == BANK and F * NQ == P and D == F and J == P

    ctx = ExitStack()
    with ctx:
        def sb(name, shape, dt=F32):
            return ctx.enter_context(nc.sbuf_tensor(name, shape, dt))

        def ps(name, shape):
            return ctx.enter_context(nc.psum_tensor(name, shape, F32))

        def sem(name):
            return ctx.enter_context(nc.semaphore(name))

        def view(ap, free):
            return bass.AP(ap.tensor, ap.offset, [list(ap.ap[0])] + [list(x) for x in free])

        ident = sb("ident", [P, P])
        ident32 = sb("ident32", [P, 2 * F])
        quad = sb("quad", [P, NQ])
        oct_ = sb("oct", [P, 8])
        half32 = sb("half32", [P, 2])
        half16 = sb("half16", [P, 2])
        sel = sb("sel", [P, 5, 2, P], F32R)
        sel16 = sb("sel16", [P, 2, P], F32R)
        w0h = sb("w0h", [P, SHIFT_TILES, J], F32R)
        w0l = sb("w0l", [P, SHIFT_TILES, J], F32R)
        w16h = sb("w16h", [P, J], F32R)
        w16m = sb("w16m", [P, 2, J], F32R)
        w1s = sb("w1s", [P, F, J])
        idc = [sb(f"idc{i}", [P, F], I32) for i in range(2)]
        emb = [sb(f"emb{i}", [P, F, D]) for i in range(2)]
        embd = [sb(f"embd{i}", [P, D, F]) for i in range(2)]
        S = [sb(f"S{i}", [P, BANK], F32R) for i in range(2)]
        e4 = [sb(f"e4{i}", [P, BANK]) for i in range(2)]
        b16 = sb("b16", [P, BANK])
        z = [sb(f"z{i}", [P, SHIFT_TILES, BANK]) for i in range(2)]
        zh = [sb(f"zh{i}", [P, SHIFT_TILES, BANK], F32R) for i in range(2)]
        zl = [sb(f"zl{i}", [P, SHIFT_TILES, BANK], F32R) for i in range(2)]
        z16 = sb("z16", [P, BANK])
        z16p = [sb(f"z16p{i}", [P, BANK], F32R) for i in range(2)]
        x1 = [sb(f"x1{i}", [P, GROUPS, NQ, D]) for i in range(2)]
        x1t = [sb(f"x1t{i}", [P, GU, P]) for i in range(2)]
        eblk = sb("eblk", [P, GROUPS, NQ, F])
        et = sb("et", [P, F, GROUPS])
        G = sb("G", [P, F, P])
        zf = sb("zf", [P, KT1, B])

        R = [ps(f"R{i}", [P, 2, BANK]) for i in range(2)]
        XO = ps("XO", [P, BANK])
        U0 = ps("U0", [P, BANK])
        U1 = ps("U1", [P, BANK])
        WA = ps("WA", [P, BANK])

        const_s = sem("const_s")
        masks_s = sem("masks_s")
        w0_loaded = sem("w0_loaded")
        w1_loaded = sem("w1_loaded")
        ids_loaded = [sem(f"ids_loaded{i}") for i in range(2)]
        gathered = [sem(f"gathered{i}") for i in range(2)]
        embd_done = sem("embd_done")
        s_transposed = sem("s_transposed")
        s_hi_done = sem("s_hi_done")
        s_lo_done = sem("s_lo_done")
        selected = sem("selected")
        e4_done = sem("e4_done")
        z_done = sem("z_done")
        zh_done = sem("zh_done")
        zl_done = sem("zl_done")
        zl3_done = sem("zl3_done")
        x1_made = sem("x1_made")
        x1_kept = sem("x1_kept")
        summed = sem("summed")
        e_transposed = sem("e_transposed")
        eblk_done = sem("eblk_done")
        x1_transposed = sem("x1_transposed")
        x1t_done = sem("x1t_done")
        g_made = sem("g_made")
        g_kept = sem("g_kept")
        x2_made = sem("x2_made")
        x2_kept = sem("x2_kept")

        def wait(eng, s, value):
            if not (isinstance(value, int) and value <= 0):
                eng.wait_ge(s, value)

        def unit(n, kind):
            return 7 * (n // 2) + ({"E4": 0, "R01": 1, "R23": 2, "REM": 3} if n % 2 == 0 else
                                   {"E4": 4, "R01": 5, "R23": 6})[kind]

        def zpos(n, kind):
            return 5 * (n // 2) + ({"01": 0, "23": 1, "16": 2} if n % 2 == 0 else {"01": 3, "23": 4})[kind]

        def e4pos(n, kind):
            return 3 * (n // 2) + ({"E4": 0, "B16": 1} if n % 2 == 0 else {"E4": 2})[kind]

        SEL, ZS, E4S = 7 * SUPERS, 5 * SUPERS, 3 * SUPERS

        G_UNITS = {n: (2 * (n - 1), 2 * (n - 1) + 1) for n in range(1, 5)}
        SUM_QUARTERS = {1: (0,), 2: (1,), 3: (2,), 5: (3,)}
        X2_FIELDS = {5: range(0, 12), 6: range(12, 23), 7: range(23, F)}
        E_QUARTERS = {5: 0, 6: 1, 7: 2}
        GATHERS = {0: 6, 1: 6, 2: 5, 3: 5, 4: 5, 5: 5}
        GATHERS_FIRST = {0: 13, 1: 4, 2: 4, 3: 4, 4: 4, 5: 3}
        assert sum(GATHERS.values()) == sum(GATHERS_FIRST.values()) == F

        SELECTION_STEPS = 2 * (SHIFT_TILES + 1 + 2)
        MASK_STEPS = 9 + SELECTION_STEPS + NQ + 7 + 2

        def tiles(eng, body):
            body(0, 0, 0, True, False)
            with eng.Fori(0, (TILES - 2) // 2) as i:
                body(2 * i + 1, 1, i, False, False)
                body(2 * i + 2, 0, i + 1, False, False)
            body(TILES - 1, 1, (TILES - 1) // 2, False, True)

        raw0, raw1 = (b[:, :, :].rearrange("p t n -> p (t n)") for b in z)
        w0a = raw0[:, 0:5 * J].rearrange("p (t j) -> p t j", j=J)
        w0b = raw0[:, 5 * J:10 * J].rearrange("p (t j) -> p t j", j=J)
        w16 = raw0[:, 10 * J:11 * J]
        wt1d = raw0[0:ND, 11 * J:11 * J + H1]
        wt1 = raw1[:, 0:KT1 * H1].rearrange("p (t n) -> p t n", t=KT1)
        W0_DMAS = 1 + 4 * (4 * SHIFT_TILES - 1) + 2
        TOWER_DMAS = 6

        PREP_HI = 2 + 2 + 2 * 2
        HB = B // 2
        vec_in = sb("vec_in", [N1 + N2 + N2, P])
        vec = sb("vec", [P, N1 + N2 + N2])
        dense_in = sb("dense_in", [P, TILES, ND])
        wt1h, wt1l = sb("wt1h", [P, KT1, H1], F32R), sb("wt1l", [P, KT1, H1], F32R)
        STACK = [slice(F * i, F * i + ND) for i in range(3)]
        NS = 2 * F + ND
        wt1s = sb("wt1s", [NS, H1], F32R)
        dTs = sb("dTs", [NS, B], F32R)
        wt2 = emb[1][:, :, :].rearrange("p f d -> p (f d)").rearrange("p (t n) -> p t n", t=N1)
        zfh, zfl = zh[0][:, 0:2, :], zl[0][:, 0:2, :]
        wt2h = zh[0][:, 2:4, :].rearrange("p a (b n) -> p (a b) n", n=H2)
        wt2l = zl[0][:, 2:4, :].rearrange("p a (b n) -> p (a b) n", n=H2)
        h1, h1h, h1l = z[0], zh[1], zl[1]
        h2 = z[1][:, 0:N2, :]
        ybuf = [e4[0][0:1, :], e4[1][0:1, :]]

        tower_loaded = sem("tower_loaded")
        wt2_loaded = sem("wt2_loaded")
        vec_transposed = sem("vec_transposed")
        dense_transposed = sem("dense_transposed")
        prep_hi = sem("prep_hi")
        prep_lo = sem("prep_lo")
        t_hi = sem("t_hi")
        t_lo = sem("t_lo")
        l1_made = sem("l1_made")
        l1_kept = sem("l1_kept")
        l1_hi = sem("l1_hi")
        l1_lo = sem("l1_lo")
        l2_made = sem("l2_made")
        l2_kept = sem("l2_kept")
        y_made = sem("y_made")
        y_kept = sem("y_kept")
        y_stored = sem("y_stored")

        block = ctx.enter_context(nc.Block())

        @block.sync
        def _(eng):
            def ids_of(k, par, uses):
                wait(eng, gathered[par], 16 * F * uses)
                eng.dma_start(idc[par][:, :], ids[bass.ds(P * k, P), :]).then_inc(ids_loaded[par], 16)

            ids_of(0, 0, 0)
            ids_of(1, 1, 0)
            eng.dma_start(wt1, w_top1[0:KT1 * P, :].rearrange("(t p) n -> p t n", p=P)).then_inc(tower_loaded, 16)
            eng.dma_start(wt1d, w_top1[KT1 * P:KT1 * P + ND, :]).then_inc(tower_loaded, 16)
            eng.dma_start(vec_in[0:N1, :], b_top1.rearrange("(t p) -> t p", p=P)).then_inc(tower_loaded, 16)
            eng.dma_start(vec_in[N1:N1 + N2, :], b_top2.rearrange("(t p) -> t p", p=P)).then_inc(tower_loaded, 16)
            eng.dma_start(vec_in[N1 + N2:, :], w_top3.rearrange("(t p) o -> t (p o)", p=P)).then_inc(tower_loaded, 16)
            eng.dma_start(dense_in[:, :, :], dense_ctx.rearrange("(t p) n -> p t n", p=P)).then_inc(tower_loaded, 16)
            for s in range(4 * SHIFT_TILES):
                t, q = s // NQ, s % NQ
                for buf, step, at, wrap in ((w0a, F + 1, s, F), (w0b, F + 1, F * s, F * F)):
                    if s == 0 and buf is w0b:
                        continue
                    n = F - s
                    eng.dma_start(buf[F * q:F * q + n, t, :], w0[at:at + step * (n - 1) + 1:step, :])\
                       .then_inc(w0_loaded, 16)
                    if s:
                        first = at + step * n - wrap
                        eng.dma_start(buf[F * q + n:F * q + F, t, :],
                                      w0[first:first + step * (s - 1) + 1:step, :]).then_inc(w0_loaded, 16)
            for buf, at in ((w0a, HALF), (w0b, F * HALF)):
                rows = w0[at:at + (F + 1) * (HALF - 1) + 1:F + 1, :]
                eng.dma_start(buf[:, SHIFT_TILES, :],
                              bass.AP(rows.tensor, rows.offset, [[0, P // HALF]] + [list(x) for x in rows.ap]))\
                   .then_inc(w0_loaded, 16)
            eng.dma_start(w1s[:, :, :], w1.rearrange("(h m) j -> m h j", m=P)).then_inc(w1_loaded, 16)
            with eng.Fori(1, TILES // 2) as i:
                ids_of(2 * i, 0, i)
                ids_of(2 * i + 1, 1, i)
            eng.wait_ge(e_transposed, TILES)
            eng.wait_ge(embd_done, 2 * TILES)
            eng.dma_start(wt2, w_top2.rearrange("(t p) n -> p t n", p=P)).then_inc(wt2_loaded, 16)
            for hb in range(2):
                eng.wait_ge(y_kept, hb + 1)
                eng.dma_start(out[hb * HB:(hb + 1) * HB, :].rearrange("b o -> o b"), ybuf[hb]).then_inc(y_stored, 16)
            eng.wait_ge(y_stored, 32)

        @block.gpsimd
        def _(eng):
            eng.memset(ident[:, :], 0.0).then_inc(const_s, 1)
            eng.wait_ge(const_s, 1)
            eng.affine_select(out=ident[:, :], in_=ident[:, :], compare_op=ALU.not_equal, fill=1.0,
                              base=0, pattern=[[-1, P]], channel_multiplier=1).then_inc(const_s, 1)

            def gather(par, fields):
                for f in fields:
                    eng.indirect_dma_start(emb[par][:, f, :], None, tables[f],
                                           bass.IndirectOffsetOnAxis(idc[par][:, f:f + 1], 0))\
                       .then_inc(gathered[par], 16)

            eng.wait_ge(ids_loaded[0], 16)
            gather(0, range(F))

            def body(k, par, uses, first, last):
                f = 0
                gathers = GATHERS_FIRST if first else GATHERS
                for n in range(CHUNKS):
                    if not last and n in gathers:
                        if n == 0:
                            eng.wait_ge(ids_loaded[1 - par], 16 * (uses + par + 1))
                            wait(eng, e_transposed, k)
                            eng.nop(nofuse=True)
                        gather(1 - par, range(f, f + gathers[n]))
                        f += gathers[n]
                    eng.wait_ge(zh_done, ZS * k + zpos(n, "23") + 1)
                    wait(eng, x1_made, CHUNKS * k + n - 1)
                    eng.tensor_tensor(zl[n % 2][:, 3, :], z[n % 2][:, 3, :], zh[n % 2][:, 3, :].bitcast(F32),
                                      ALU.subtract).then_inc(zl3_done, 1)

            tiles(eng, body)

        @block.scalar
        def _(eng):
            def copy(dst, src):
                return eng.activation(dst, src, ACT.Copy)

            def by_d(k, par, uses, part):
                if part == 0:
                    eng.wait_ge(gathered[par], 16 * F * (uses + 1))
                    wait(eng, s_transposed, SUPERS * (k - 1))
                ds = slice(0, 2 * CD) if part == 0 else slice(2 * CD, D)
                copy(embd[par][:, ds, :], emb[par][:, :, ds].rearrange("p f d -> p d f")).then_inc(embd_done, 1)

            def s_hi(k, sg):
                eng.wait_ge(s_transposed, SUPERS * k + sg + 1)
                wait(eng, selected, SEL * k + 7 * (sg - 1))
                copy(S[sg % 2][0:2 * F, :], U0[0:2 * F, :]).then_inc(s_hi_done, 1)

            def x1t_copy(tile, u):
                eng.wait_ge(x1_transposed, UNITS * tile + u + 1)
                if u > 1:
                    eng.wait_ge(g_made, UNITS * tile + u - 1)
                copy(x1t[u % 2][:, :, :], U0[:, :]).then_inc(x1t_done, 1)

            def g_copy(tile, u):
                eng.wait_ge(g_made, UNITS * tile + u + 1)
                copy(G[:, :, :].rearrange("p h (q g) -> p h q g", q=NQ)[:, :, :, GU * u:GU * u + GU],
                     U1[:, :].rearrange("p (g q h) -> p h q g", g=GU, q=NQ)).then_inc(g_kept, 1)

            def x1_copy(tile, m, par):
                eng.wait_ge(x1_made, CHUNKS * tile + m + 1)
                d = 2 * CD * (m // 2) + m % 2
                copy(x1[par][:, :, :, d:d + 2 * CD - 1:2].rearrange("p g q d -> p q g d"),
                     XO[:, :].rearrange("p (d q g) -> p q g d", d=CD, q=NQ)).then_inc(x1_kept, 1)

            def x2_copy(tile):
                eng.wait_ge(x2_made, tile + 1)
                copy(zf[:, 1, bass.ds(P * tile, P)], WA[:, 0:P]).then_inc(x2_kept, 1)

            def e_quarter(k, q):
                eng.wait_ge(e_transposed, k + 1)
                rows = slice(F * q, F * q + F)
                copy(eblk[rows, :, q, :], et[rows, :, :].rearrange("p h g -> p g h")).then_inc(eblk_done, 1)

            def body(k, par, uses, first, last):
                for n in range(CHUNKS):
                    units = G_UNITS.get(n, ()) if not first else ()
                    eng.wait_ge(selected, SEL * k + unit(n, "E4") + 1)
                    wait(eng, z_done, ZS * k + (zpos(n - 2, "23") + 1 if n >= 2 else zpos(n - 2 + CHUNKS, "23") + 1 - ZS))
                    copy(e4[n % 2][:, :], R[unit(n, "E4") % 2][:, 0, :]).then_inc(e4_done, 1)
                    if units:
                        x1t_copy(k - 1, units[0])
                    if n == 0 and not first:
                        by_d(k, par, uses, 1)
                    if n in E_QUARTERS:
                        e_quarter(k, E_QUARTERS[n])
                    eng.wait_ge(z_done, ZS * k + zpos(n, "01") + 1)
                    wait(eng, x1_made, CHUNKS * k + n - 1)
                    copy(zh[n % 2][:, 0:2, :], z[n % 2][:, 0:2, :]).then_inc(zh_done, 1)
                    if n % 2 == 0:
                        eng.wait_ge(selected, SEL * k + unit(n, "REM") + 1)
                        wait(eng, z_done, ZS * k + zpos(n, "16") + 1 - 5)
                        copy(b16[:, :], R[unit(n, "REM") % 2][:, 0, :]).then_inc(e4_done, 1)
                    if units:
                        g_copy(k - 1, units[0])
                        x1t_copy(k - 1, units[1])
                    if n == CHUNKS - 1 and not last:
                        s_hi(k + 1, 0)
                    if n == 0 and not first:
                        x1_copy(k - 1, CHUNKS - 1, 1 - par)
                    eng.wait_ge(z_done, ZS * k + zpos(n, "23") + 1)
                    copy(zh[n % 2][:, 2:4, :], z[n % 2][:, 2:4, :]).then_inc(zh_done, 1)
                    if n % 2 == 0:
                        eng.wait_ge(z_done, ZS * k + zpos(n, "16") + 1)
                        wait(eng, x1_made, CHUNKS * k + n - 2)
                        copy(z16p[n // 2 % 2][:, :], z16[:, :]).then_inc(zh_done, 1)
                    if units and n % 2 == 0:
                        g_copy(k - 1, units[1])
                    if n:
                        x1_copy(k, n - 1, par)
                    if units and n % 2:
                        g_copy(k - 1, units[1])
                    if n in (0, 2, 4):
                        s_hi(k, n // 2 + 1)
                    if n == CHUNKS - 2 and not last:
                        by_d(k + 1, 1 - par, uses + par, 0)
                    if n == CHUNKS - 1:
                        e_quarter(k, NQ - 1)
                        if not first:
                            x2_copy(k - 1)

            eng.wait_ge(vec_transposed, 1)
            copy(vec[:, :], WA[:, 0:N1 + 2 * N2]).then_inc(prep_hi, 1)
            eng.wait_ge(tower_loaded, 16 * TOWER_DMAS)
            copy(wt1h[:, :, :], wt1).then_inc(prep_hi, 1)
            eng.wait_ge(masks_s, 8)
            for rows in (STACK[0], STACK[2]):
                copy(wt1s[rows, :], wt1d).then_inc(prep_hi, 1)
            for hb in range(2):
                eng.wait_ge(dense_transposed, hb + 1)
                for rows in STACK[0:2]:
                    copy(dTs[rows, hb * HB:(hb + 1) * HB], R[0][0:ND, hb, :]).then_inc(prep_hi, 1)

            by_d(0, 0, 0, 0)
            s_hi(0, 0)
            by_d(0, 0, 0, 1)
            tiles(eng, body)

            def features(hb):
                copy(zfh, zf[:, :, hb * HB:(hb + 1) * HB]).then_inc(t_hi, 1)

            def hidden1(hb, a):
                eng.wait_ge(l1_made, N1 * hb + a + 1)
                wait(eng, l1_lo, N1 * (hb - 1) + a + 1)
                eng.activation(h1[:, a, :], R[1 - a // 2][:, a % 2, :], ACT.Relu, bias=vec[:, a:a + 1])\
                   .then_inc(l1_kept, 1)

            def hidden2(hb, a):
                eng.wait_ge(l2_made, N2 * hb + a + 1)
                wait(eng, y_made, hb)
                eng.activation(h2[:, a, :], (U0, U1)[a][:, :], ACT.Relu, bias=vec[:, N1 + a:N1 + a + 1])\
                   .then_inc(l2_kept, 1)

            def result(hb):
                eng.wait_ge(y_made, hb + 1)
                copy(ybuf[hb], XO[0:1, :]).then_inc(y_kept, 1)

            t = TILES - 1
            eng.wait_ge(x1_made, CHUNKS * TILES - 1)
            eng.wait_ge(summed, NQ * (TILES // 2))
            eng.wait_ge(x2_kept, TILES // 2)
            features(0)
            x1_copy(t, CHUNKS - 1, t % 2)
            x1t_copy(t, 0)
            for u in range(UNITS):
                g_copy(t, u)
                if u + 1 < UNITS:
                    x1t_copy(t, u + 1)
                if u == 0:
                    eng.wait_ge(wt2_loaded, 16)
                    copy(wt2h, wt2).then_inc(t_hi, 1)
                if u % 2:
                    hidden1(0, u // 2)
            x2_copy(t)
            eng.wait_ge(summed, NQ * TILES)
            eng.wait_ge(x2_kept, TILES)
            eng.wait_ge(t_lo, 1)
            features(1)
            for a in range(N2):
                hidden2(0, a)
            for a in range(N1):
                hidden1(1, a)
            result(0)
            for a in range(N2):
                hidden2(1, a)
            result(1)

        @block.vector
        def _(eng):
            eng.wait_ge(const_s, 2)
            for c in range(2):
                eng.tensor_reduce(ident32[:, F * c:F * c + F], ident[:, :].rearrange("p (a h) -> p h a", h=F), AX.X, ALU.add).then_inc(masks_s, 1)
            eng.tensor_reduce(quad[:, :], ident[:, :].rearrange("p (q h) -> p q h", h=F), AX.X, ALU.add).then_inc(masks_s, 1)
            eng.tensor_reduce(oct_[:, :], ident[:, :].rearrange("p (q h) -> p q h", h=HALF), AX.X, ALU.add).then_inc(masks_s, 1)
            eng.wait_ge(masks_s, 4)
            eng.tensor_reduce(half32[:, :], quad[:, :].rearrange("p (a x) -> p x a", x=2), AX.X, ALU.add).then_inc(masks_s, 1)
            eng.tensor_reduce(half16[:, :], oct_[:, :].rearrange("p (a x) -> p x a", x=2), AX.X, ALU.add).then_inc(masks_s, 1)
            eng.memset(wt1s[:, :].bitcast(F32), 0.0).then_inc(masks_s, 1)
            eng.memset(dTs[:, :].bitcast(F32), 0.0).then_inc(masks_s, 1)
            eng.memset(eblk[:, :, :, :], 0.0).then_inc(masks_s, 1)
            eng.wait_ge(masks_s, 6)
            for x in range(2):
                for t in range(SHIFT_TILES + 1):
                    src = (view(ident32[:, NQ * t:NQ * t + 1], [[1, NQ], [1, F]]) if t < SHIFT_TILES else
                           view(ident32[:, 0:1], [[0, NQ], [1, F]]))
                    eng.tensor_scalar(sel[:, t, x, :].rearrange("p (s h) -> p s h", h=F), src,
                                      half32[:, x:x + 1], None, ALU.mult).then_inc(masks_s, 1)
                for r in range(2):
                    dst = sel16[:, r, :].rearrange("p (c x h) -> p c x h", x=2, h=HALF)[:, :, x, :]
                    eng.tensor_scalar(dst, view(ident32[:, HALF * r:HALF * r + 1], [[0, NQ], [1, HALF]]),
                                      half32[:, x:x + 1], None, ALU.mult).then_inc(masks_s, 1)
            eng.wait_ge(w0_loaded, 16 * W0_DMAS)
            for q in range(1, NQ):
                eng.tensor_tensor(w0a[F * q:F * q + F, 0, :], w0a[F * q:F * q + F, 0, :],
                                  w0b[F * q:F * q + F, 0, :], ALU.add).then_inc(masks_s, 1)
            eng.tensor_tensor(w0a[:, 1:, :], w0a[:, 1:, :], w0b[:, 1:, :], ALU.add).then_inc(masks_s, 1)
            done = 9 + SELECTION_STEPS + NQ
            eng.wait_ge(masks_s, done)
            eng.tensor_copy(w0h[:, :, :], w0a[:, 0:SHIFT_TILES, :]).then_inc(masks_s, 1)
            eng.tensor_copy(w16h[:, :], w0a[:, SHIFT_TILES, :]).then_inc(masks_s, 1)
            eng.wait_ge(masks_s, done + 2)
            eng.tensor_tensor(w0l[:, :, :], w0a[:, 0:SHIFT_TILES, :], w0h[:, :, :].bitcast(F32), ALU.subtract).then_inc(masks_s, 1)
            for q in range(NQ):
                rows = slice(F * q, F * q + F)
                if q % 2:
                    eng.tensor_tensor(w16[rows, :], w0a[rows, SHIFT_TILES, :], w16h[rows, :].bitcast(F32), ALU.subtract).then_inc(masks_s, 1)
                else:
                    eng.tensor_copy(w16[rows, :], w16h[rows, :].bitcast(F32)).then_inc(masks_s, 1)
            eng.wait_ge(masks_s, done + 7)
            assert done + 7 + 2 == MASK_STEPS
            for x in range(2):
                eng.tensor_scalar(w16m[:, x, :], w16[:, :], half16[:, x:x + 1], None, ALU.mult).then_inc(masks_s, 1)

            def s_lo(k, sg):
                eng.wait_ge(s_hi_done, SUPERS * k + sg + 1)
                eng.tensor_tensor(S[sg % 2][2 * F:P, :], U0[0:2 * F, :], S[sg % 2][0:2 * F, :].bitcast(F32),
                                  ALU.subtract).then_inc(s_lo_done, 1)

            def sum_d(tile, q, par):
                eng.tensor_reduce(zf[:, 0, bass.ds(P * tile + F * q, F)], x1[par][:, :, q, :], AX.X, ALU.add)\
                   .then_inc(summed, 1)

            def shift16(k, n):
                eng.wait_ge(e4_done, E4S * k + e4pos(n, "B16") + 1)
                wait(eng, zh_done, ZS * k + zpos(n, "16") + 1 - 5)
                wait(eng, zl_done, ZS * k + zpos(n, "16") + 1 - 5)
                eng.tensor_tensor(z16[:, :], R[unit(n, "REM") % 2][:, 1, :], b16[:, :], ALU.mult).then_inc(z_done, 1)

            def body(k, par, uses, first, last):
                for n in range(CHUNKS):
                    b = n % 2
                    eng.wait_ge(e4_done, E4S * k + e4pos(n, "E4") + 1)
                    eng.wait_ge(selected, SEL * k + unit(n, "R01") + 1)
                    back = ZS * k + (zpos(n - 2, "23") if n >= 2 else zpos(n - 2 + CHUNKS, "23") - ZS) + 1
                    wait(eng, zh_done, back)
                    wait(eng, zl_done, back)
                    e4b = view(e4[b][:, 0:1], [[0, 2], [1, BANK]])
                    eng.tensor_tensor(z[b][:, 0:2, :], R[unit(n, "R01") % 2][:, :, :], e4b, ALU.mult).then_inc(z_done, 1)
                    eng.wait_ge(selected, SEL * k + unit(n, "R23") + 1)
                    wait(eng, zl3_done, CHUNKS * k + n - 1)
                    eng.tensor_tensor(z[b][:, 2:4, :], R[unit(n, "R23") % 2][:, :, :], e4b, ALU.mult).then_inc(z_done, 1)
                    if not first and n in G_UNITS and n % 2 == 0:
                        shift16(k, n)
                    eng.wait_ge(zh_done, ZS * k + zpos(n, "01") + 1)
                    wait(eng, x1_made, CHUNKS * k + n - 1)
                    eng.tensor_tensor(zl[b][:, 0:2, :], z[b][:, 0:2, :], zh[b][:, 0:2, :].bitcast(F32), ALU.subtract).then_inc(zl_done, 1)
                    if (first or n not in G_UNITS) and n % 2 == 0:
                        shift16(k, n)
                    if not first and n in SUM_QUARTERS:
                        eng.wait_ge(x1_kept, CHUNKS * k)
                        for q in SUM_QUARTERS[n]:
                            sum_d(k - 1, q, 1 - par)
                    if n == CHUNKS - 1 and not last:
                        s_lo(k + 1, 0)
                    eng.wait_ge(zh_done, ZS * k + zpos(n, "23") + 1)
                    eng.tensor_tensor(zl[b][:, 2, :], z[b][:, 2, :], zh[b][:, 2, :].bitcast(F32), ALU.subtract).then_inc(zl_done, 1)
                    if n % 2 == 0:
                        eng.wait_ge(zh_done, ZS * k + zpos(n, "16") + 1)
                        rows = slice(P // 2, P)
                        eng.tensor_tensor(z16p[n // 2 % 2][rows, :], z16[rows, :],
                                          z16p[n // 2 % 2][rows, :].bitcast(F32), ALU.subtract).then_inc(zl_done, 1)
                    if n == 4:
                        eng.wait_ge(gathered[par], 16 * F * (uses + 1))
                        wait(eng, eblk_done, NQ * k)
                        eng.transpose(et[:, :, :].rearrange("p h g -> p (h g)"),
                                      emb[par][:, :, :].rearrange("p h d -> p (h d)")).then_inc(e_transposed, 1)
                    if n in (0, 2, 4):
                        s_lo(k, n // 2 + 1)

            eng.wait_ge(prep_hi, PREP_HI)
            eng.tensor_tensor(wt1l[:, :, :], wt1, wt1h[:, :, :].bitcast(F32), ALU.subtract).then_inc(prep_lo, 1)
            eng.tensor_tensor(wt1s[STACK[1], :], wt1d, wt1s[0:ND, :].bitcast(F32), ALU.subtract).then_inc(prep_lo, 1)
            for hb in range(2):
                cols = slice(hb * HB, (hb + 1) * HB)
                eng.tensor_tensor(dTs[STACK[2], cols], R[0][0:ND, hb, :], dTs[0:ND, cols].bitcast(F32), ALU.subtract).then_inc(prep_lo, 1)
            eng.wait_ge(prep_lo, 4)
            eng.wait_ge(masks_s, MASK_STEPS)

            s_lo(0, 0)
            tiles(eng, body)

            def features(hb):
                eng.tensor_tensor(zfl, zf[:, :, hb * HB:(hb + 1) * HB], zfh.bitcast(F32), ALU.subtract).then_inc(t_lo, 1)

            def hidden1(hb, a):
                eng.wait_ge(l1_kept, N1 * hb + a + 1)
                wait(eng, l2_made, N2 * hb)
                eng.tensor_copy(h1h[:, a, :], h1[:, a, :]).then_inc(l1_hi, 1)
                eng.wait_ge(l1_hi, N1 * hb + a + 1)
                eng.tensor_tensor(h1l[:, a, :], h1[:, a, :], h1h[:, a, :].bitcast(F32), ALU.subtract).then_inc(l1_lo, 1)

            eng.wait_ge(t_hi, 1)
            features(0)
            eng.wait_ge(x1_kept, CHUNKS * TILES)
            for q in range(NQ):
                sum_d(TILES - 1, q, (TILES - 1) % 2)
            eng.wait_ge(t_hi, 2)
            eng.tensor_tensor(wt2l, wt2, wt2h.bitcast(F32), ALU.subtract).then_inc(t_lo, 1)
            for a in range(N1):
                hidden1(0, a)
            eng.wait_ge(t_hi, 3)
            eng.wait_ge(l1_made, N1)
            features(1)
            for a in range(N1):
                hidden1(1, a)

        @block.tensor
        def _(eng):
            eng.wait_ge(const_s, 2)

            def s_transposes(k, sg, par, first):
                if sg >= 2 and not first:
                    eng.wait_ge(x1t_done, UNITS * (k - 1) + {2: 4, 3: UNITS}[sg])
                elif sg or not isinstance(k, int) or k:
                    eng.wait_ge(s_lo_done, SUPERS * k + sg)
                if sg < 2:
                    eng.wait_ge(embd_done, 2 * k + sg + 1)
                eng.nop(nofuse=True)
                for dq in range(CD):
                    d = 2 * CD * sg + 2 * dq
                    t = eng.transpose(U0[0:2 * F, P * dq:P * dq + P],
                                      embd[par][:, d:d + 2, :].rearrange("p d h -> p (d h)"), ident[:, :])
                t.then_inc(s_transposed, 1)

            def select(k, n, kind, banks):
                u = unit(n, kind)
                src = S[n // 2 % 2][:, :]
                for i, lhsT in enumerate(banks):
                    m = eng.matmul(R[u % 2][:, i, :], lhsT, src, start=True, stop=True)
                m.then_inc(selected, 1)

            def products(k, n, t):
                b = n % 2
                eng.matmul(XO[:, :], w0h[:, t, :], zh[b][:, t, :], start=(t == 0), stop=False)
                eng.matmul(XO[:, :], w0l[:, t, :], zh[b][:, t, :], start=False, stop=False)
                m = eng.matmul(XO[:, :], w0h[:, t, :], zl[b][:, t, :], start=False, stop=(t == SHIFT_TILES - 1))
                return m

            def products_a(k, n):
                eng.wait_ge(zh_done, ZS * k + zpos(n, "01") + 1)
                eng.wait_ge(zl_done, ZS * k + zpos(n, "01") + 1)
                wait(eng, x1_kept, CHUNKS * k + n)
                products(k, n, 0)
                products(k, n, 1)

            def products_b(k, n):
                rem = 1 if n % 2 == 0 else 0
                eng.wait_ge(zh_done, ZS * k + zpos(n, "23") + 1 + rem)
                eng.wait_ge(zl_done, ZS * k + zpos(n, "23") + 1 + rem)
                products(k, n, 2)
                eng.matmul(XO[:, :], w16m[:, n % 2, :], z16p[n // 2 % 2][:, :], start=False, stop=False)

            def products_c(k, n):
                eng.wait_ge(zl3_done, CHUNKS * k + n + 1)
                products(k, n, 3).then_inc(x1_made, 1)

            def x1_transposes(tile, u, par):
                for i in range(GU):
                    t = eng.transpose(U0[:, P * i:P * i + P],
                                      x1[par][:, GU * u + i, :, :].rearrange("p q d -> p (q d)"), ident[:, :])
                t.then_inc(x1_transposed, 1)

            def g_products(tile, u):
                eng.wait_ge(x1t_done, UNITS * tile + u + 1)
                if u:
                    eng.wait_ge(g_kept, UNITS * tile + u)
                for i in range(GU):
                    m = eng.matmul(U1[:, P * i:P * i + P], x1t[u % 2][:, i, :],
                                   eblk[:, GU * u + i, :, :].rearrange("p q h -> p (q h)"), start=True, stop=True)
                m.then_inc(g_made, 1)

            def x2_products(fields):
                for h in fields:
                    m = eng.matmul(WA[:, 0:P], w1s[:, h, :], G[:, h, :], start=(h == 0), stop=(h == F - 1))
                return m

            def body(k, par, uses, first, last):
                for n in range(CHUNKS):
                    units = G_UNITS.get(n, ()) if not first else ()
                    main = (k, n - 1) if n else None if first else (k - 1, CHUNKS - 1)
                    if n % 2 == 0:
                        eng.wait_ge(s_lo_done, SUPERS * k + n // 2 + 1)
                        wait(eng, z_done, ZS * k + (zpos(n - 1, "01") + 1 if n else zpos(CHUNKS - 1, "01") + 1 - ZS))
                    else:
                        wait(eng, z_done, ZS * k + zpos(n - 1, "23") + 1)
                    select(k, n, "E4", [sel[:, SHIFT_TILES, n % 2, :]])
                    if units and n == 1:
                        products_a(*main)
                    if n % 2 == 0:
                        wait(eng, z_done, ZS * k + (zpos(n - 1, "23") + 1 if n else 0))
                    else:
                        eng.wait_ge(z_done, ZS * k + zpos(n - 1, "16") + 1)
                    select(k, n, "R01", [sel[:, 0, n % 2, :], sel[:, 1, n % 2, :]])
                    if units and n % 2 == 0:
                        eng.wait_ge(x1t_done, UNITS * (k - 1) + units[0])
                        x1_transposes(k - 1, units[0], 1 - par)
                    if not first and n != 1:
                        products_a(*main)
                    if units and n == 3:
                        eng.wait_ge(s_lo_done, SUPERS * k + n // 2 + 2)
                        x1_transposes(k - 1, units[0], 1 - par)
                    eng.wait_ge(e4_done, E4S * k + e4pos(n, "E4") + 1)
                    select(k, n, "R23", [sel[:, 2, n % 2, :], sel[:, 3, n % 2, :]])
                    if n == CHUNKS - 1 and not last:
                        s_transposes(k + 1, 0, 1 - par, first)
                    if first and n:
                        products_a(*main)
                    if units and n == 1:
                        eng.wait_ge(x1_kept, CHUNKS * k)
                        eng.wait_ge(eblk_done, NQ * k)
                        eng.wait_ge(s_lo_done, SUPERS * k + n // 2 + 2)
                        x1_transposes(k - 1, units[0], 1 - par)
                    if main and (n % 2 or not units):
                        products_b(*main)
                    if n % 2 == 0:
                        eng.wait_ge(z_done, ZS * k + zpos(n, "01") + 1)
                        select(k, n, "REM", [sel16[:, 0, :], sel16[:, 1, :]])
                    if units:
                        g_products(k - 1, units[0])
                        eng.wait_ge(x1t_done, UNITS * (k - 1) + units[1])
                        x1_transposes(k - 1, units[1], 1 - par)
                    if units and n % 2 == 0:
                        products_b(*main)
                        g_products(k - 1, units[1])
                    if main:
                        products_c(*main)
                    if units and n % 2:
                        g_products(k - 1, units[1])
                    if n in (0, 2, 4):
                        s_transposes(k, n // 2 + 1, par, first)
                    if not first and n in X2_FIELDS:
                        if n == 5:
                            eng.wait_ge(g_kept, UNITS * k)
                        m = x2_products(X2_FIELDS[n])
                        if n == CHUNKS - 1:
                            m.then_inc(x2_made, 1)

            eng.wait_ge(tower_loaded, 16 * TOWER_DMAS)
            NV = N1 + 2 * N2
            eng.transpose(WA[:, 0:NV], vec_in[:, :], ident[0:NV, 0:NV]).then_inc(vec_transposed, 1)
            for t in range(TILES):
                m = eng.transpose(R[0][0:ND, t // 4, P * (t % 4):P * (t % 4) + P], dense_in[:, t, :], ident[:, :])
                if t % 4 == 3:
                    m.then_inc(dense_transposed, 1)
            s_transposes(0, 0, 0, True)
            eng.wait_ge(masks_s, MASK_STEPS)
            eng.wait_ge(prep_lo, 4)
            eng.wait_ge(w1_loaded, 16)
            tiles(eng, body)

            def hidden1(hb, a):
                cols, half = slice(P * a, P * a + P), slice(hb * HB, (hb + 1) * HB)
                pairs = []
                for c in range(KT1):
                    pairs += [(wt1h[:, c, cols], zfh[:, c, :]), (wt1l[:, c, cols], zfh[:, c, :]),
                              (wt1h[:, c, cols], zfl[:, c, :])]
                return pairs + [(wt1s[:, cols], dTs[:, half])]

            def hidden1_products(hb, a, part):
                pairs = hidden1(hb, a)
                for i in part:
                    m = eng.matmul(R[1 - a // 2][:, a % 2, :], *pairs[i], start=(i == 0), stop=(i == len(pairs) - 1))
                    if i == len(pairs) - 1:
                        m.then_inc(l1_made, 1)

            def hidden2_products(hb):
                for a in range(N2):
                    o = (U0, U1)[a][:, :]
                    cols = slice(P * a, P * a + P)
                    wait(eng, l2_kept, N2 * (hb - 1) + a + 1)
                    eng.wait_ge(t_lo, 2)
                    for c in range(N1):
                        eng.wait_ge(l1_lo, N1 * hb + c + 1)
                        eng.matmul(o, wt2h[:, c, cols], h1h[:, c, :], start=(c == 0), stop=False)
                        eng.matmul(o, wt2l[:, c, cols], h1h[:, c, :], start=False, stop=False)
                        m = eng.matmul(o, wt2h[:, c, cols], h1l[:, c, :], start=False, stop=(c == N1 - 1))
                    m.then_inc(l2_made, 1)

            def result(hb):
                wait(eng, y_kept, hb)
                for a in range(N2):
                    eng.wait_ge(l2_kept, N2 * hb + a + 1)
                    m = eng.matmul(XO[0:1, :], vec[:, N1 + N2 + a:N1 + N2 + a + 1], h2[:, a, :], start=(a == 0), stop=(a == N2 - 1))
                m.then_inc(y_made, 1)

            t = TILES - 1
            products_a(t, CHUNKS - 1)
            products_b(t, CHUNKS - 1)
            products_c(t, CHUNKS - 1)
            eng.wait_ge(x1_kept, CHUNKS * TILES)
            eng.wait_ge(eblk_done, NQ * TILES)
            x1_transposes(t, 0, t % 2)
            eng.wait_ge(t_lo, 1)
            eng.wait_ge(z_done, ZS * TILES)
            for u in range(UNITS):
                hidden1_products(0, u // 2, range(4) if u % 2 == 0 else range(4, 7))
                g_products(t, u)
                if u + 1 < UNITS:
                    eng.wait_ge(x1t_done, UNITS * t + u + 1)
                    x1_transposes(t, u + 1, t % 2)
            eng.wait_ge(g_kept, UNITS * TILES)
            x2_products(range(F)).then_inc(x2_made, 1)
            hidden2_products(0)
            eng.wait_ge(t_lo, 3)
            for a in range(N1):
                eng.wait_ge(l1_kept, a + 1)
                hidden1_products(1, a, range(7))
            result(0)
            hidden2_products(1)
            result(1)


N_TABLES = 32
_INS = (["dense_ctx", "ids"] + [f"tbl_{f}" for f in range(N_TABLES)] +
        ["W_top1", "b_top1", "W_top2", "b_top2", "W_top3", "L0_rec_W0", "L0_rec_W1"])


def kernel(**inputs):
    import numpy as np
    import concourse.bacc as bacc
    from concourse.bass_utils import run_bass_kernel_spmd

    nc = bacc.Bacc("TRN2", target_bir_lowering=False, num_devices=1)
    arrays, aps = {}, {}
    for name in _INS:
        a = np.ascontiguousarray(inputs[name])
        arrays[f"in_{name}"] = a
        aps[name] = nc.dram_tensor(f"in_{name}", a.shape, mybir.dt.from_np(a.dtype), kind="ExternalInput").ap()
    batch = inputs["ids"].shape[0]
    out = nc.dram_tensor("out_y", (batch, 1), F32, kind="ExternalOutput").ap()
    dlrm_cin_tower(nc, aps["dense_ctx"], aps["ids"], [aps[f"tbl_{f}"] for f in range(N_TABLES)],
                   aps["W_top1"], aps["b_top1"], aps["W_top2"], aps["b_top2"], aps["W_top3"],
                   aps["L0_rec_W0"], aps["L0_rec_W1"], out)
    r = run_bass_kernel_spmd(nc, [arrays], core_ids=[0])
    return r.results[0]["out_y"]
```
